# Optimizing a Trainium2 kernel written in Bass

```python
import numpy as np
import jax
import jax.numpy as jnp

def _softmax(x, axis=-1):
    return jax.nn.softmax(x, axis=axis)

def _gelu(x):
    return jax.nn.gelu(x, approximate=True)

def _silu(x):
    return jax.nn.silu(x)

def _sigmoid(x):
    return jax.nn.sigmoid(x)

def _layernorm(x, axis=-1, eps=1e-05):
    m = jnp.mean(x, axis=axis, keepdims=True)
    v = jnp.var(x, axis=axis, keepdims=True)
    return (x - m) / jnp.sqrt(v + eps)

def _scatter_add(tgt, idx, src, axis=0):
    return tgt.at[idx].add(src)

def _segment_sum(src, seg, n):
    return jax.ops.segment_sum(src, seg, n)
kernel_name = 'mk_decoder_postln_d1_seqx_r4_56c701'

def setup_inputs(seed: int=0):
    np.random.seed(seed)
    _w = jnp.asarray

    def _rec_inputs():
        import jax
        import jax.numpy as jnp
        _rk = jax.random.key(seed)
        x = -0.0005207 + 1.001 * jax.random.normal(jax.random.fold_in(_rk, 1), (1, 2048, 256), jnp.float32)
        _lenS = 2048 - jax.random.randint(jax.random.fold_in(_rk, 7), (1,), 0, max(1, 2048 // 4) + 1, jnp.int32)
        _lenS2 = 1601 - jax.random.randint(jax.random.fold_in(_rk, 8), (1,), 0, max(1, 1601 // 4) + 1, jnp.int32)
        _ctx_1024P = jax.random.normal(jax.random.fold_in(_rk, 11), (1, 16, 256), jnp.float32)
        _ctx_1024c = jax.random.dirichlet(jax.random.fold_in(_rk, 511), 0.3 * jnp.ones((16,), jnp.float32), (1, 1601))
        _ctx_1024t = jnp.einsum('bsk,bkd->bsd', _ctx_1024c, _ctx_1024P)
        _ctx_1024t = _ctx_1024t * jax.lax.rsqrt(jnp.mean(jnp.square(_ctx_1024t)) + 1e-12) * 0.953939
        ctx_1024 = -5.72187e-05 + 0.999849 * (_ctx_1024t + 0.3 * jax.random.normal(jax.random.fold_in(_rk, 611), (1, 1601, 256), jnp.float32))
        return (x, ctx_1024)
    x, ctx_1024 = _rec_inputs()

    def _L0_attn_setup():
        import jax, jax.numpy as jnp
        import numpy as np
        B, S, D, K = (4, 1024, 256, 64)
        key = jax.random.key(seed)
        kx, kq, kk, kv, ko = jax.random.split(key, 5)
        scale = 1.0 / np.sqrt(D)
        return {'x': jax.random.normal(kx, (B, S, D), dtype=jnp.float32), 'Wq': jax.random.uniform(kq, (K, D), dtype=jnp.float32, minval=-scale, maxval=scale), 'Wk': jax.random.uniform(kk, (K, D), dtype=jnp.float32, minval=-scale, maxval=scale), 'Wv': jax.random.uniform(kv, (K, D), dtype=jnp.float32, minval=-scale, maxval=scale), 'Wo': jax.random.uniform(ko, (D, K), dtype=jnp.float32, minval=-1.0 / np.sqrt(K), maxval=1.0 / np.sqrt(K))}
    _L0_attn_all = _L0_attn_setup()
    _L0_attn_in = {k: v for k, v in _L0_attn_all.items() if k in ('Wq', 'Wk', 'Wv', 'Wo')}
    del _L0_attn_all

    def _L0_xattn_setup():
        import jax, jax.numpy as jnp
        import numpy as np
        key = jax.random.key(seed)
        ks = jax.random.split(key, 5)
        b, n_q, n_kv = (16, 128, 1024)
        query_dim, context_dim, heads, dim_head = (256, 256, 16, 64)
        inner = heads * dim_head
        x = jax.random.normal(ks[0], (b, n_q, query_dim), dtype=jnp.float32)
        context = jax.random.normal(ks[1], (b, n_kv, context_dim), dtype=jnp.float32)
        Wq = jax.random.normal(ks[2], (query_dim, inner), dtype=jnp.float32) * query_dim ** (-0.5)
        Wkv = jax.random.normal(ks[3], (context_dim, 2 * inner), dtype=jnp.float32) * context_dim ** (-0.5)
        Wout = jax.random.normal(ks[4], (inner, query_dim), dtype=jnp.float32) * inner ** (-0.5)
        bout = jnp.zeros((query_dim,), dtype=jnp.float32)
        return {'x': x, 'context': context, 'Wq': Wq, 'Wkv': Wkv, 'Wout': Wout, 'bout': bout}
    _L0_xattn_all = _L0_xattn_setup()
    _L0_xattn_in = {k: v for k, v in _L0_xattn_all.items() if k in ('Wq', 'Wkv', 'Wout', 'bout')}
    del _L0_xattn_all

    def _L0_ffn_setup():
        import jax, jax.numpy as jnp
        import numpy as np
        D_IN, D_HID = (256, 1024)

        def _ternary(key, shape):
            return jax.random.randint(key, shape, -1, 2).astype(jnp.float32)

        def _tlin(x, w, s):
            return jnp.einsum('bsi,oi->bso', x, w) * s
        key = jax.random.key(seed)
        ks = jax.random.split(key, 12)
        inv = lambda fan: 1.0 / np.sqrt(fan).astype(np.float32)
        return {'x': jax.random.normal(ks[0], (4, 512, D_IN), dtype=jnp.float32), 'w1_w': _ternary(ks[1], (D_HID, D_IN)), 'w1_s': jax.random.uniform(ks[2], (D_HID,), dtype=jnp.float32) * inv(D_IN), 'w2_w': _ternary(ks[3], (D_HID, D_IN)), 'w2_s': jax.random.uniform(ks[4], (D_HID,), dtype=jnp.float32) * inv(D_IN), 'h1_w': _ternary(ks[5], (D_HID, D_HID)), 'h1_s': jax.random.uniform(ks[6], (D_HID,), dtype=jnp.float32) * inv(D_HID), 'h2_w': _ternary(ks[7], (D_HID, D_HID)), 'h2_s': jax.random.uniform(ks[8], (D_HID,), dtype=jnp.float32) * inv(D_HID), 'w3_w': _ternary(ks[9], (D_IN, D_HID)), 'w3_s': jax.random.uniform(ks[10], (D_IN,), dtype=jnp.float32) * inv(D_HID)}
    _L0_ffn_all = _L0_ffn_setup()
    _L0_ffn_in = {k: v for k, v in _L0_ffn_all.items() if k in ('w1_w', 'w1_s', 'w2_w', 'w2_s', 'h1_w', 'h1_s', 'h2_w', 'h2_s', 'w3_w', 'w3_s')}
    del _L0_ffn_all
    return {'x': x, 'ctx_1024': ctx_1024, 'L0_attn_Wq': _L0_attn_in['Wq'], 'L0_attn_Wk': _L0_attn_in['Wk'], 'L0_attn_Wv': _L0_attn_in['Wv'], 'L0_attn_Wo': _L0_attn_in['Wo'], 'L0_xattn_Wq': _L0_xattn_in['Wq'], 'L0_xattn_Wkv': _L0_xattn_in['Wkv'], 'L0_xattn_Wout': _L0_xattn_in['Wout'], 'L0_xattn_bout': _L0_xattn_in['bout'], 'L0_ffn_w1_w': _L0_ffn_in['w1_w'], 'L0_ffn_w1_s': _L0_ffn_in['w1_s'], 'L0_ffn_w2_w': _L0_ffn_in['w2_w'], 'L0_ffn_w2_s': _L0_ffn_in['w2_s'], 'L0_ffn_h1_w': _L0_ffn_in['h1_w'], 'L0_ffn_h1_s': _L0_ffn_in['h1_s'], 'L0_ffn_h2_w': _L0_ffn_in['h2_w'], 'L0_ffn_h2_s': _L0_ffn_in['h2_s'], 'L0_ffn_w3_w': _L0_ffn_in['w3_w'], 'L0_ffn_w3_s': _L0_ffn_in['w3_s']}

def reference(x, ctx_1024, L0_attn_Wq, L0_attn_Wk, L0_attn_Wv, L0_attn_Wo, L0_xattn_Wq, L0_xattn_Wkv, L0_xattn_Wout, L0_xattn_bout, L0_ffn_w1_w, L0_ffn_w1_s, L0_ffn_w2_w, L0_ffn_w2_s, L0_ffn_h1_w, L0_ffn_h1_s, L0_ffn_h2_w, L0_ffn_h2_s, L0_ffn_w3_w, L0_ffn_w3_s):
    import jax
    import jax.numpy as jnp

    def _L0_attn_ref(x, Wq, Wk, Wv, Wo):
        import jax, jax.numpy as jnp
        import numpy as np
        B, S, D, K = (4, 1024, 256, 64)
        Q = jax.nn.elu(x @ Wq.T) + 1.0
        Kf = jax.nn.elu(x @ Wk.T) + 1.0
        V = x @ Wv.T
        KV_sum = jnp.cumsum(Kf[..., :, None] * V[..., None, :], axis=1)
        K_sum = jnp.cumsum(Kf, axis=1)
        num = jnp.einsum('bsk,bskm->bsm', Q, KV_sum)
        den = jnp.einsum('bsk,bsk->bs', Q, K_sum)[..., None]
        out = num / (den + 1e-06)
        return out @ Wo.T

    def _L0_xattn_ref(x, context, Wq, Wkv, Wout, bout):
        import jax, jax.numpy as jnp
        import numpy as np
        heads, dim_head = (16, 64)
        b, n_q, _ = x.shape
        n_kv = context.shape[1]
        scale = dim_head ** (-0.5)
        q = x @ Wq
        kv = context @ Wkv
        k, v = jnp.split(kv, 2, axis=-1)

        def split_heads(t):
            bb, n, _ = t.shape
            return t.reshape(bb, n, heads, dim_head).transpose(0, 2, 1, 3)
        q, k, v = map(split_heads, (q, k, v))
        i_idx = jnp.arange(n_q)[:, None]
        j_idx = jnp.arange(n_kv)[None, :]
        mask = j_idx % n_q == i_idx
        sim = jnp.einsum('bhid,bhjd->bhij', q, k) * scale
        max_neg = -jnp.finfo(sim.dtype).max
        sim = jnp.where(mask[None, None, :, :], sim, max_neg)
        attn = jax.nn.softmax(sim, axis=-1)
        out = jnp.einsum('bhij,bhjd->bhid', attn, v)
        out = out.transpose(0, 2, 1, 3).reshape(b, n_q, heads * dim_head)
        return out @ Wout + bout

    def _L0_ffn_ref(x, w1_w, w1_s, w2_w, w2_s, h1_w, h1_s, h2_w, h2_s, w3_w, w3_s):
        import jax, jax.numpy as jnp
        import numpy as np
        D_IN, D_HID = (256, 1024)

        def _ternary(key, shape):
            return jax.random.randint(key, shape, -1, 2).astype(jnp.float32)

        def _tlin(x, w, s):
            return jnp.einsum('bsi,oi->bso', x, w) * s
        h = jax.nn.silu(_tlin(x, w1_w, w1_s)) * _tlin(x, w2_w, w2_s)
        h = jax.nn.gelu(_tlin(h, h1_w, h1_s), approximate=False)
        h = jax.nn.gelu(_tlin(h, h2_w, h2_s), approximate=False)
        return _tlin(h, w3_w, w3_s)
    x = _layernorm(x + _L0_attn_ref(x, L0_attn_Wq, L0_attn_Wk, L0_attn_Wv, L0_attn_Wo), axis=-1)
    x = _layernorm(x + _L0_xattn_ref(x, ctx_1024, L0_xattn_Wq, L0_xattn_Wkv, L0_xattn_Wout, L0_xattn_bout), axis=-1)
    x = _layernorm(x + _L0_ffn_ref(x, L0_ffn_w1_w, L0_ffn_w1_s, L0_ffn_w2_w, L0_ffn_w2_s, L0_ffn_h1_w, L0_ffn_h1_s, L0_ffn_h2_w, L0_ffn_h2_s, L0_ffn_w3_w, L0_ffn_w3_s), axis=-1)
    return x

_drawn_inputs = setup_inputs


def setup_inputs(seed=0):
    import zlib

    import numpy as np

    out = dict(_drawn_inputs(seed))
    spreads = {'L0_xattn_bout': (0.0, 0.1)}
    factors = {'L0_attn_Wq': 8.0,
     'L0_attn_Wk': 8.0,
     'L0_attn_Wv': 3.565,
     'L0_attn_Wo': 3.83,
     'L0_ffn_w1_w': 8.0,
     'L0_ffn_w1_s': 8.0,
     'L0_ffn_w2_w': 8.0,
     'L0_ffn_w2_s': 8.0,
     'L0_ffn_h1_w': 8.0,
     'L0_ffn_h1_s': 8.0,
     'L0_ffn_h2_w': 8.0,
     'L0_ffn_h2_s': 8.0,
     'L0_ffn_w3_w': 8.0,
     'L0_ffn_w3_s': 8.0}
    for name, (base, spread) in spreads.items():
        noise = np.random.default_rng([zlib.crc32(name.encode()), seed]).standard_normal(out[name].shape)
        drawn = base * np.exp(spread * noise) if base else spread * noise
        out[name] = jnp.asarray(drawn.astype(out[name].dtype))
    for name, factor in factors.items():
        out[name] = (out[name] * factor).astype(out[name].dtype)
    return out
```

```python
from contextlib import ExitStack

import concourse.bass as bass
from concourse import mybir

ALU = mybir.AluOpType
ACT = mybir.ActivationFunctionType
AX = mybir.AxisListType
F32 = mybir.dt.float32
F32R = mybir.dt.float32r
I32 = mybir.dt.int32

P = 128
S = 2048
SC = 1601
D = 256
DK = D // P
KH = 64
INNER = 1024
IK = INNER // P
F = 1024
FK = F // P
T = 512
CHUNKS = S // T
TT = T // P
EPS = 1e-5
DEN_EPS = 1e-6

W1, W2, H1, H2, W3 = 0, DK * F, 2 * DK * F, 2 * DK * F + FK * F, 2 * DK * F + 2 * FK * F
WCOLS = W3 + FK * D
PIECES = 4 * CHUNKS
PCOLS = WCOLS // PIECES
assert PCOLS * PIECES == WCOLS

GATE_SLOTS = FK
HID_SLOTS = FK // 2
OUT_SLOTS = TT // 2
SLOTS = GATE_SLOTS + 2 * HID_SLOTS + OUT_SLOTS
TILES = 3 * FK
HF = 4
LO_PIECES = GATE_SLOTS + 2 * HID_SLOTS * 4 + OUT_SLOTS * 4
assert SLOTS % 2 == 0


def decoder_layer(nc, x_tok, x_feat, ctx_feat, wqkv_d, wo_d, wv_d, wout_d, bout_d, ffn_w, scales_d, w3s_d, out):
    with ExitStack() as ctx:
        def sem(name):
            return ctx.enter_context(nc.semaphore(name))

        def keep(name, shape, dt=F32):
            return ctx.enter_context(nc.sbuf_tensor(name, shape, dt))

        W = keep("W", [P, WCOLS], F32R)
        x2_all = keep("x2_all", [P, CHUNKS, TT * D])
        x2T_all = keep("x2T_all", [P, DK, S])
        scales = keep("scales", [P, 4 * FK])
        w3s = keep("w3s", [P, D])
        stats = keep("stats", [P, TT, 6])
        mv = keep("mv", [P, TT, 2])
        veps = keep("veps", [P, TT])
        rstd = keep("rstd", [P, TT])
        eps = keep("eps", [P, TT])
        minus_half = keep("minus_half", [P, TT])
        unequal = keep("unequal", [P, PIECES])
        unequal_sum = keep("unequal_sum", [P, 1])
        ones = keep("ones", [P, 1])
        flag = keep("flag", [1, 1], I32)

        def area(stack):
            return lambda name, shape, dt=F32: stack.enter_context(nc.sbuf_tensor(name, shape, dt))

        with ExitStack() as attention:
            sb = area(attention)
            stage = [sb(f"stage{i}", [P, PCOLS]) for i in range(2)]
            ctx_full = sb("ctx_full", [P, DK, S])
            ctx_sum = sb("ctx_sum", [P, DK])
            ctx_mean = sb("ctx_mean", [P, DK])
            ctx_chunk = sb("ctx_chunk", [P, DK, T])
            xT = sb("xT", [P, DK, T])
            xt = sb("xt", [P, TT, D])
            wqkv = sb("wqkv", [P, DK, 3 * KH])
            wo = sb("wo", [KH, D])
            wvo = sb("wvo", [P, DK, D])
            bout = sb("bout", [P, D])
            den_pick = sb("den_pick", [KH + 1, 1])
            mask = sb("mask", [P, TT, P])
            ident = sb("ident", [P, P])
            e_qk = sb("e_qk", [P, T])
            r_qk = sb("r_qk", [P, T])
            e_k = sb("e_k", [P, TT, KH])
            r_k = sb("r_k", [P, TT, KH])
            qT = sb("qT", [KH, T])
            kT = sb("kT", [KH, T])
            kv1 = sb("kv1", [P, TT, 2 * KH + 1])
            sT = sb("sT", [P, TT, P])
            state = sb("state", [KH, TT + 1, KH + 1])
            numT = sb("numT", [KH + 1, T])
            den = sb("den", [P, TT])
            rden = sb("rden", [P, TT])
            with ExitStack() as early:
                wv = area(early)("wv", [P, IK, D])
                wout = area(early)("wout", [P, IK, D])
            res1 = sb("res1", [P, TT, D])
            ub = sb("ub", [P, TT, D])
            res2 = sb("res2", [P, TT, D])
            x2 = sb("x2", [P, TT, D])

        with ExitStack() as feed_forward:
            sb = area(feed_forward)
            hf = [sb(f"hf{i}", [P, T]) for i in range(HF)]
            xs = [sb(f"xs_{p}", [P, DK, T], F32R) for p in ("hi", "lo")]
            w_again = sb("w_again", [P, T])
            w_lo = sb("w_lo", [P, T], F32R)
            h1 = [sb(f"h1_{p}", [P, FK, T], F32R) for p in ("hi", "lo")]
            with ExitStack() as late:
                fin = area(late)("fin", [P, OUT_SLOTS, 2, D])
            h2 = [sb(f"h2_{p}", [P, FK, T], F32R) for p in ("hi", "lo")]

        ps = ctx.enter_context(nc.psum_tensor("ps", [P, 8, 512], F32))
        QK, KV, SC_B, Y_B, ND_B, U_B = 0, 1, 2, 3, 5, 6
        kv_ps = ps[:, KV, :].rearrange("p (t c) -> p t c", t=TT)
        s_ps = ps[:, SC_B, :].rearrange("p (t c) -> p t c", t=TT)
        y_ps = ps[:, Y_B:Y_B + 2, :].rearrange("p b (t c) -> p (b t) c", t=2)
        u_ps = ps[:, U_B:U_B + 2, :].rearrange("p b (t c) -> p (b t) c", t=2)
        delta_ps = ps[0:KH, ND_B, 0:TT * (KH + 1)].rearrange("p (t c) -> p t c", t=TT)
        numT_ps = ps[0:KH + 1, ND_B, :]
        den_ps = ps[:, ND_B, 0:TT]
        wvo_ps = [ps[:, U_B + c, 0:D] for c in range(DK)]
        x2T_ps = [ps[:, Y_B + c, :] for c in range(DK)]
        flag_ps = ps[0:1, SC_B, 0:1]

        got_xT, got_xt, got_wqkv, got_wo = sem("got_xT"), sem("got_xt"), sem("got_wqkv"), sem("got_wo")
        got_wv, got_wout, got_ctx, got_bout = sem("got_wv"), sem("got_wout"), sem("got_ctx"), sem("got_bout")
        got_scales, got_w3s = sem("got_scales"), sem("got_w3s")
        got_stage = [sem("got_stage0"), sem("got_stage1")]
        got_again, stored = sem("got_again"), sem("stored")
        ident_zero, ident_made = sem("ident_zero"), sem("ident_made")
        mask_one, mask_made = sem("mask_one"), sem("mask_made")
        dve_consts, pool_consts = sem("dve_consts"), sem("pool_consts")
        wvo_done, qkv_done, sd_done, u_done = sem("wvo_done"), sem("qkv_done"), sem("sd_done"), sem("u_done")
        num_done, y_done, tr_done, flag_sum = sem("num_done"), sem("y_done"), sem("tr_done"), sem("flag_sum")
        wvo_copied, qkv_acted, u_copied = sem("wvo_copied"), sem("qkv_acted"), sem("u_copied")
        num_copied, x2T_copied, w_rounded = sem("num_copied"), sem("x2T_copied"), sem("w_rounded")
        ctx_summed, mean_made, tail_filled = sem("ctx_summed"), sem("mean_made"), sem("tail_filled")
        sT_made, state_step, elu_made = sem("sT_made"), sem("state_step"), sem("elu_made")
        den_step, res1_made, res2_made = sem("den_step"), sem("res1_made"), sem("res2_made")
        stats1_made, mv1_made, x1_made = sem("stats1_made"), sem("mv1_made"), sem("x1_made")
        stats2_made, mv2_made, x2_made = sem("stats2_made"), sem("mv2_made"), sem("x2_made")
        w_looked, flag_step, flag_made = sem("w_looked"), sem("flag_step"), sem("flag_made")
        ctx_copied, ub_made, x2_kept = sem("ctx_copied"), sem("ub_made"), sem("x2_kept")
        veps_made, rstd_made = sem("veps_made"), sem("rstd_made")
        slot_done = sem("slot_done")
        xs_hi_made, xs_ready = sem("xs_hi_made"), sem("xs_ready")
        silu_made, gate_made = sem("silu_made"), sem("gate_made")
        gelu_made = sem("gelu_made")
        hi_made, h_ready = sem("hi_made"), sem("h_ready")
        out_read = sem("out_read")
        out_added, stats3_made, mv3_made, out_made = sem("out_added"), sem("stats3_made"), sem("mv3_made"), sem("out_made")
        lo_made, lo_used = sem("lo_made"), sem("lo_used")

        block = ctx.enter_context(nc.Block())

        @block.sync
        def _(sp):
            sp.dma_start(wqkv[:, :, :], wqkv_d).then_inc(got_wqkv, 16)
            sp.dma_start(xT[:, :, :], x_feat[0]).then_inc(got_xT, 16)
            sp.dma_start(wv[:, :, :], wv_d).then_inc(got_wv, 16)
            sp.dma_start(wout[:, :, :], wout_d).then_inc(got_wout, 16)

            def load_piece(n, i):
                g = 4 * n + i
                if not (isinstance(n, int) and g < 2):
                    sp.wait_ge(w_looked, g - 1)
                sp.dma_start(stage[i % 2][:, :], ffn_w[:, bass.ds(g * PCOLS, PCOLS)]).then_inc(got_stage[i % 2], 16)

            def loads(n, last=False):
                if not last:
                    sp.wait_ge(qkv_done, n + 1)
                    sp.dma_start(xT[:, :, :], x_feat[bass.ds(n + 1, 1)].rearrange("a p k t -> (a p) k t")).then_inc(got_xT, 16)
                for i in range(4):
                    load_piece(n, i)
                if not last:
                    sp.wait_ge(res1_made, n + 1)
                    sp.dma_start(xt[:, :, :], x_tok[bass.ds(n + 1, 1)].rearrange("a p t d -> (a p) t d")).then_inc(got_xt, 16)

            loads(0)
            with sp.Fori(1, CHUNKS - 1) as n:
                loads(n)
            loads(CHUNKS - 1, last=True)

            def store(n, pair):
                sp.wait_ge(out_made, OUT_SLOTS * n + pair + 1)
                c = pair * 2 * D
                sp.dma_start(out[bass.ds(n, 1), :, c:c + 2 * D].rearrange("a p c -> (a p) c"),
                             x2_all[:, bass.ds(n, 1), c:c + 2 * D].rearrange("p a c -> p (a c)")).then_inc(stored, 16)

            gates = ffn_w[:, W1:H1].rearrange("p (k o) -> p k o", o=F)
            hidden = [ffn_w[:, h:h + FK * F].rearrange("p (k o) -> p k o", o=F) for h in (H1, H2)]

            def lo_pieces():
                for m in range(GATE_SLOTS):
                    yield gates[:, :, m * P:(m + 1) * P]
                for w in hidden:
                    for m in range(FK):
                        for k in (0, FK // 2):
                            yield w[:, k:k + FK // 2, m * P:(m + 1) * P]
                for _ in range(OUT_SLOTS):
                    for k in range(0, FK, 2):
                        yield ffn_w[:, W3 + k * D:W3 + (k + 2) * D]

            sp.wait_ge(flag_made, 1)
            finer = sp.value_load(flag[0:1, 0:1], min_val=0, max_val=1)
            with sp.If(finer > 0):
                with sp.Fori(0, CHUNKS) as n:
                    for i, piece in enumerate(lo_pieces()):
                        if i:
                            sp.wait_ge(lo_made, LO_PIECES * n + i)
                        dst = w_again[:, :]
                        if len(piece.shape) == 3:
                            dst = dst.rearrange("p (k o) -> p k o", o=P)
                        sp.dma_start(dst, piece).then_inc(got_again, 16)
                    sp.wait_ge(lo_made, LO_PIECES * n + LO_PIECES)
                    for pair in range(OUT_SLOTS):
                        store(n, pair)
            with sp.Else():
                with sp.Fori(0, CHUNKS) as n:
                    for pair in range(OUT_SLOTS):
                        store(n, pair)
            sp.wait_ge(stored, 16 * OUT_SLOTS * CHUNKS)

        @block.gpsimd
        def _(pool):
            nc.gpsimd.memset(ident[:, :], 0.0).then_inc(ident_zero, 1)
            nc.gpsimd.memset(mask[:, :, :], 1.0).then_inc(mask_one, 1)
            nc.gpsimd.memset(eps[:, :], EPS)
            nc.gpsimd.memset(minus_half[:, :], -0.5).then_inc(pool_consts, 1)
            pool.wait_ge(ident_zero, 1)
            nc.gpsimd.affine_select(out=ident[:, :], in_=ident[:, :], compare_op=ALU.not_equal, fill=1.0,
                                    base=0, pattern=[[-1, P]], channel_multiplier=1).then_inc(ident_made, 1)
            pool.wait_ge(mask_one, 1)
            nc.gpsimd.affine_select(out=mask[:, :, :], in_=mask[:, :, :], compare_op=ALU.is_ge, fill=0.0,
                                    base=0, pattern=[[0, TT], [1, P]], channel_multiplier=-1).then_inc(mask_made, 1)
            pool.wait_ge(pool_consts, 1)
            pool.wait_ge(got_ctx, 16)

            def copy_ctx(n):
                nc.gpsimd.tensor_copy(ctx_chunk[:, :, :], ctx_full[:, :, bass.ds(n * T, T)]).then_inc(ctx_copied, 1)

            def inverse_root(count, mv_made, at_least, c0, c1):
                pool.wait_ge(mv_made, at_least)
                nc.gpsimd.tensor_tensor(veps[:, c0:c1], mv[:, c0:c1, 1], eps[:, c0:c1], ALU.add).then_inc(veps_made, 1)
                pool.wait_ge(veps_made, count)
                nc.gpsimd.tensor_tensor(rstd[:, c0:c1], veps[:, c0:c1], minus_half[:, c0:c1], ALU.pow).then_inc(rstd_made, 1)

            def chunk(n, last=False):
                if not last:
                    pool.wait_ge(u_done, n + 1)
                    copy_ctx(n + 1)
                pool.wait_ge(u_copied, n + 1)
                nc.gpsimd.tensor_tensor(ub[:, :, :], ub[:, :, :], bout[:, :].unsqueeze(1).to_broadcast([P, TT, D]),
                                        ALU.add).then_inc(ub_made, 1)
                inverse_root(2 * n + 1, mv1_made, n + 1, 0, TT)
                inverse_root(2 * n + 2, mv2_made, n + 1, 0, TT)
                pool.wait_ge(x2_made, n + 1)
                nc.gpsimd.tensor_copy(x2_all[:, bass.ds(n, 1), :].rearrange("p a c -> p (a c)"),
                                      x2[:, :, :].rearrange("p t d -> p (t d)")).then_inc(x2_kept, 1)

            copy_ctx(0)
            pool.wait_ge(got_bout, 16)
            pool.wait_ge(tail_filled, 1)
            chunk(0)
            with pool.Fori(1, CHUNKS - 1) as n:
                chunk(n)
            chunk(CHUNKS - 1, last=True)

            with pool.Fori(0, CHUNKS) as n:
                for pair in range(OUT_SLOTS):
                    count = OUT_SLOTS * n + pair + 1
                    inverse_root(count + 2 * CHUNKS, mv3_made, count, 2 * pair, 2 * pair + 2)

        @block.scalar
        def _(act):
            act.dma_start(ctx_full[:, :, 0:SC], ctx_feat).then_inc(got_ctx, 16)
            act.dma_start(xt[:, :, :], x_tok[0]).then_inc(got_xt, 16)
            act.dma_start(wo[:, :], wo_d).then_inc(got_wo, 16)
            act.dma_start(bout[:, :], bout_d.partition_broadcast(P)).then_inc(got_bout, 16)
            act.dma_start(w3s[:, :], w3s_d.partition_broadcast(P)).then_inc(got_w3s, 16)
            act.dma_start(scales[:, :], scales_d).then_inc(got_scales, 16)

            def qkv_parts(m):
                act.wait_ge(qkv_done, m + 1)
                nc.scalar.activation(e_qk[:, :], ps[:, QK, :], ACT.Exp)
                nc.scalar.activation(r_qk[:, :], ps[:, QK, :], ACT.Relu)
                nc.scalar.activation(e_k[:, :, :], kv_ps[:, :, 0:KH], ACT.Exp)
                nc.scalar.activation(r_k[:, :, :], kv_ps[:, :, 0:KH], ACT.Relu)
                nc.scalar.copy(kv1[:, :, KH:2 * KH], kv_ps[:, :, KH:2 * KH]).then_inc(qkv_acted, 1)

            def round_piece(n, i):
                g = 4 * n + i
                act.wait_ge(got_stage[i % 2], 16 * (2 * n + i // 2 + 1))
                nc.scalar.copy(W[:, bass.ds(g * PCOLS, PCOLS)], stage[i % 2][:, :]).then_inc(w_rounded, 1)

            def keep_x2T(n):
                act.wait_ge(tr_done, n + 1)
                for k in range(DK):
                    c = nc.scalar.copy(x2T_all[:, k, bass.ds(n * T, T)], x2T_ps[k])
                c.then_inc(x2T_copied, 1)

            def chunk(n, first=False, last=False):
                round_piece(n, 0)
                act.wait_ge(u_done, n + 1)
                if not first:
                    act.wait_ge(res2_made, n)
                nc.scalar.copy(ub[:, :, :], u_ps).then_inc(u_copied, 1)
                round_piece(n, 1)
                act.wait_ge(num_done, n + 1)
                nc.scalar.copy(numT[:, :], numT_ps).then_inc(num_copied, 1)
                if not first:
                    keep_x2T(n - 1)
                if not last:
                    act.wait_ge(elu_made, n + 1)
                    qkv_parts(n + 1)
                round_piece(n, 2)
                round_piece(n, 3)

            qkv_parts(0)
            act.wait_ge(wvo_done, 1)
            for c in range(DK):
                cp = nc.scalar.copy(wvo[:, c, :], wvo_ps[c])
            cp.then_inc(wvo_copied, 1)
            chunk(0, first=True)
            with act.Fori(1, CHUNKS - 1) as n:
                chunk(n)
            chunk(CHUNKS - 1, last=True)
            keep_x2T(CHUNKS - 1)

            def split_x_hi(n):
                nc.scalar.copy(xs[0][:, :, :], x2T_all[:, :, bass.ds(n * T, T)]).then_inc(xs_hi_made, 1)

            def hi(n, tile):
                h = h1 if tile // FK != 1 else h2
                nc.scalar.copy(h[0][:, tile % FK, :], hf[tile % HF][:, :]).then_inc(hi_made, 1)

            def ffn(n, split_next):
                for m in range(GATE_SLOTS + 1):
                    if m < GATE_SLOTS:
                        act.wait_ge(slot_done, SLOTS * n + m + 1)
                        if m >= HF:
                            act.wait_ge(h_ready, TILES * n + m - HF + 1)
                        nc.scalar.activation(hf[m % HF][:, :], ps[:, 2 * (m % 2), :], ACT.Silu,
                                             scale=scales[:, m:m + 1]).then_inc(silu_made, 1)
                    if m:
                        act.wait_ge(gate_made, GATE_SLOTS * n + m)
                        hi(n, m - 1)
                for layer in range(2):
                    if layer == 1 and split_next:
                        act.wait_ge(slot_done, SLOTS * n + GATE_SLOTS)
                        split_x_hi(n + 1)
                    for j in range(HID_SLOTS):
                        slot = GATE_SLOTS + layer * HID_SLOTS + j
                        act.wait_ge(slot_done, SLOTS * n + slot + 1)
                        for b in range(2):
                            tile = FK * (layer + 1) + 2 * j + b
                            act.wait_ge(h_ready, TILES * n + tile - HF + 1)
                            s = FK * (layer + 2) + 2 * j + b
                            g = nc.scalar.activation(hf[tile % HF][:, :], ps[:, 2 * (slot % 2) + b, :], ACT.Gelu,
                                                     scale=scales[:, s:s + 1])
                            g.then_inc(gelu_made, 1)
                        for b in range(2):
                            tile = FK * (layer + 1) + 2 * j + b
                            act.wait_ge(gelu_made, 2 * FK * n + tile - FK + 1)
                            hi(n, tile)

            act.wait_ge(x2T_copied, CHUNKS)
            act.wait_ge(got_scales, 16)
            split_x_hi(0)
            with act.Fori(0, CHUNKS - 1) as n:
                ffn(n, True)
            ffn(CHUNKS - 1, False)

        @block.vector
        def _(dve):
            nc.vector.memset(den_pick[0:KH, :], 0.0)
            nc.vector.memset(den_pick[KH:KH + 1, :], 1.0)
            nc.vector.memset(ones[:, :], 1.0)
            nc.vector.memset(kv1[:, :, 2 * KH:2 * KH + 1], 1.0).then_inc(dve_consts, 1)

            def elu(m):
                dve.wait_ge(qkv_acted, m + 1)
                nc.vector.scalar_tensor_tensor(qT[:, :], e_qk[0:KH, :], 1.0, r_qk[0:KH, :], ALU.min, ALU.add)
                nc.vector.scalar_tensor_tensor(kT[:, :], e_qk[KH:P, :], 1.0, r_qk[KH:P, :], ALU.min, ALU.add)
                nc.vector.scalar_tensor_tensor(kv1[:, :, 0:KH], e_k[:, :, :], 1.0, r_k[:, :, :],
                                               ALU.min, ALU.add).then_inc(elu_made, 1)

            def look(n, i):
                g = 4 * n + i
                dve.wait_ge(w_rounded, g + 1)
                nc.vector.scalar_tensor_tensor(stage[i % 2][:, :], stage[i % 2][:, :], 1.0,
                                               W[:, bass.ds(g * PCOLS, PCOLS)].bitcast(F32), ALU.mult, ALU.not_equal,
                                               accum_out=unequal[:, bass.ds(g, 1)]).then_inc(w_looked, 1)

            def moments(src, at_least, made, stats_made, mv_made, count):
                dve.wait_ge(made, at_least)
                for t in range(TT):
                    s = nc.vector.bn_stats(stats[:, t, :], src[:, t, :])
                s.then_inc(stats_made, 1)
                dve.wait_ge(dve_consts, 1)
                dve.wait_ge(stats_made, count)
                for t in range(TT):
                    s = nc.vector.bn_aggr(mv[:, t, :], stats[:, t, :])
                s.then_inc(mv_made, 1)

            def norm(dst, src, made):
                for t in range(TT):
                    s = nc.vector.tensor_scalar(dst[:, t, :], src[:, t, :], mv[:, t, 0:1], rstd[:, t:t + 1],
                                                ALU.subtract, ALU.mult)
                s.then_inc(made, 1)

            def chunk(n, first=False, last=False):
                dve.wait_ge(sd_done, n + 1)
                nc.vector.tensor_tensor(sT[:, :, :], s_ps, mask[:, :, :], ALU.mult).then_inc(sT_made, 1)
                if not first:
                    dve.wait_ge(state_step, (TT + 1) * n)
                    nc.vector.tensor_copy(state[:, 0, :], state[:, TT, :]).then_inc(state_step, 1)
                else:
                    nc.vector.memset(state[:, 0, :], 0.0).then_inc(state_step, 1)
                for t in range(TT):
                    dve.wait_ge(state_step, (TT + 1) * n + t + 1)
                    nc.vector.tensor_tensor(state[:, t + 1, :], delta_ps[:, t, :], state[:, t, :],
                                            ALU.add).then_inc(state_step, 1)
                look(n, 0)
                if not last:
                    elu(n + 1)
                look(n, 1)
                dve.wait_ge(y_done, n + 1)
                nc.vector.tensor_scalar(den[:, :], den_ps, DEN_EPS, None, ALU.add).then_inc(den_step, 1)
                dve.wait_ge(den_step, 2 * n + 1)
                nc.vector.reciprocal(rden[:, :], den[:, :]).then_inc(den_step, 1)
                dve.wait_ge(den_step, 2 * n + 2)
                dve.wait_ge(got_xt, 16 * (n + 1))
                for t in range(TT):
                    s = nc.vector.scalar_tensor_tensor(res1[:, t, :], y_ps[:, t, :], rden[:, t:t + 1], xt[:, t, :],
                                                       ALU.mult, ALU.add)
                s.then_inc(res1_made, 1)
                moments(res1, n + 1, res1_made, stats1_made, mv1_made, n + 1)
                look(n, 2)
                dve.wait_ge(rstd_made, 2 * n + 1)
                norm(res1, res1, x1_made)
                dve.wait_ge(x1_made, n + 1)
                dve.wait_ge(ub_made, n + 1)
                nc.vector.tensor_tensor(res2[:, :, :], res1[:, :, :], ub[:, :, :], ALU.add).then_inc(res2_made, 1)
                moments(res2, n + 1, res2_made, stats2_made, mv2_made, n + 1)
                look(n, 3)
                dve.wait_ge(rstd_made, 2 * n + 2)
                if not first:
                    dve.wait_ge(x2_kept, n)
                    dve.wait_ge(tr_done, n)
                norm(x2, res2, x2_made)

            dve.wait_ge(got_ctx, 16)
            nc.vector.tensor_reduce(ctx_sum[:, :], ctx_full[:, :, 0:SC], axis=AX.X, op=ALU.add).then_inc(ctx_summed, 1)
            elu(0)
            dve.wait_ge(ctx_summed, 1)
            nc.vector.tensor_scalar(ctx_mean[:, :], ctx_sum[:, :], 1.0 / SC, None, ALU.mult).then_inc(mean_made, 1)
            dve.wait_ge(mean_made, 1)
            for k in range(DK):
                s = nc.vector.tensor_copy(ctx_full[:, k, SC:S], ctx_mean[:, k:k + 1].to_broadcast([P, S - SC]))
            s.then_inc(tail_filled, 1)
            dve.wait_ge(mask_made, 1)
            chunk(0, first=True)
            with dve.Fori(1, CHUNKS - 1) as n:
                chunk(n)
            chunk(CHUNKS - 1, last=True)

            dve.wait_ge(w_looked, PIECES)
            nc.vector.tensor_reduce(unequal_sum[:, :], unequal[:, :], axis=AX.X, op=ALU.add).then_inc(flag_step, 1)
            dve.wait_ge(flag_sum, 1)
            nc.vector.tensor_scalar(flag[:, :], flag_ps, 0.0, None, ALU.is_gt).then_inc(flag_made, 1)
            dve.wait_ge(flag_made, 1)
            finer = dve.value_load(flag[0:1, 0:1], min_val=0, max_val=1)
            dve.wait_ge(x2T_copied, CHUNKS)
            dve.sem_inc(out_read, OUT_SLOTS)

            def split_x_lo(n):
                dve.wait_ge(xs_hi_made, n + 1)
                nc.vector.tensor_tensor(xs[1][:, :, :], x2T_all[:, :, bass.ds(n * T, T)],
                                        xs[0][:, :, :].bitcast(F32), ALU.subtract).then_inc(xs_ready, 1)

            def lo(n, tile):
                h = h1 if tile // FK != 1 else h2
                dve.wait_ge(hi_made, TILES * n + tile + 1)
                nc.vector.tensor_tensor(h[1][:, tile % FK, :], hf[tile % HF][:, :],
                                        h[0][:, tile % FK, :].bitcast(F32), ALU.subtract).then_inc(h_ready, 1)

            def weights_lo(n, i, hi_part):
                dve.wait_ge(got_again, 16 * (LO_PIECES * n + i + 1))
                if i:
                    dve.wait_ge(lo_used, LO_PIECES * n + i)
                a, b = w_again[:, :], w_lo[:, :]
                if len(hi_part.shape) == 3:
                    a, b = (v.rearrange("p (k o) -> p k o", o=P) for v in (a, b))
                nc.vector.tensor_tensor(b, a, hi_part.bitcast(F32), ALU.subtract).then_inc(lo_made, 1)

            gates_w = W[:, W1:H1].rearrange("p (k o) -> p k o", o=F)
            hidden_w = [W[:, h:h + FK * F].rearrange("p (k o) -> p k o", o=F) for h in (H1, H2)]

            def ffn(n, split_next, finer):
                for m in range(GATE_SLOTS + 1):
                    if m < GATE_SLOTS:
                        if finer:
                            weights_lo(n, m, gates_w[:, :, m * P:(m + 1) * P])
                        dve.wait_ge(silu_made, GATE_SLOTS * n + m + 1)
                        nc.vector.scalar_tensor_tensor(hf[m % HF][:, :], ps[:, 2 * (m % 2) + 1, :],
                                                       scales[:, FK + m:FK + m + 1], hf[m % HF][:, :],
                                                       ALU.mult, ALU.mult).then_inc(gate_made, 1)
                    if m:
                        lo(n, m - 1)
                i = GATE_SLOTS
                for layer in range(2):
                    if layer == 1 and split_next:
                        split_x_lo(n + 1)
                    for j in range(HID_SLOTS):
                        for b in range(2):
                            m = 2 * j + b
                            if finer:
                                for k in (0, FK // 2):
                                    weights_lo(n, i, hidden_w[layer][:, k:k + FK // 2, m * P:(m + 1) * P])
                                    i += 1
                        for b in range(2):
                            lo(n, FK * (layer + 1) + 2 * j + b)
                for pair in range(OUT_SLOTS):
                    if finer:
                        for k in range(0, FK, 2):
                            weights_lo(n, i, W[:, W3 + k * D:W3 + (k + 2) * D])
                            i += 1
                    slot = SLOTS - OUT_SLOTS + pair
                    bank = 2 * (slot % 2)
                    count = OUT_SLOTS * n + pair + 1
                    c = pair * 2 * D
                    resid = x2_all[:, bass.ds(n, 1), c:c + 2 * D].rearrange("p a (t d) -> p (a t) d", t=2)
                    dve.wait_ge(slot_done, SLOTS * n + slot + 1)
                    nc.vector.tensor_tensor(fin[:, pair, :, :], ps[:, bank:bank + 2, 0:D],
                                            w3s[:, :].unsqueeze(1).to_broadcast([P, 2, D]), ALU.mult).then_inc(out_read, 1)
                    dve.wait_ge(out_read, count + OUT_SLOTS)
                    nc.vector.tensor_tensor(fin[:, pair, :, :], fin[:, pair, :, :], resid, ALU.add).then_inc(out_added, 1)
                    dve.wait_ge(out_added, count)
                    for t in range(2):
                        s = nc.vector.bn_stats(stats[:, 2 * pair + t, :], fin[:, pair, t, :])
                    s.then_inc(stats3_made, 1)
                    dve.wait_ge(dve_consts, 1)
                    dve.wait_ge(stats3_made, count)
                    for t in range(2):
                        s = nc.vector.bn_aggr(mv[:, 2 * pair + t, :], stats[:, 2 * pair + t, :])
                    s.then_inc(mv3_made, 1)
                    dve.wait_ge(rstd_made, 2 * CHUNKS + count)
                    for t in range(2):
                        tt = 2 * pair + t
                        s = nc.vector.tensor_scalar(
                            x2_all[:, bass.ds(n, 1), tt * D:(tt + 1) * D].rearrange("p a c -> p (a c)"),
                            fin[:, pair, t, :], mv[:, tt, 0:1], rstd[:, tt:tt + 1], ALU.subtract, ALU.mult)
                    s.then_inc(out_made, 1)

            dve.wait_ge(got_w3s, 16)
            dve.wait_ge(x2_kept, CHUNKS)
            split_x_lo(0)
            with dve.If(finer > 0):
                with dve.Fori(0, CHUNKS - 1) as n:
                    ffn(n, True, True)
                ffn(CHUNKS - 1, False, True)
            with dve.Else():
                with dve.Fori(0, CHUNKS - 1) as n:
                    ffn(n, True, False)
                ffn(CHUNKS - 1, False, False)

        @block.tensor
        def _(pe):
            def qkv(m):
                pe.wait_ge(got_xT, 16 * (m + 1))
                for k in range(DK):
                    nc.tensor.matmul(ps[:, QK, :], wqkv[:, k, 0:2 * KH], xT[:, k, :], start=(k == 0), stop=(k == DK - 1))
                for t in range(TT):
                    for k in range(DK):
                        mm = nc.tensor.matmul(kv_ps[:, t, :], xT[:, k, t * P:(t + 1) * P], wqkv[:, k, KH:3 * KH],
                                              start=(k == 0), stop=(k == DK - 1))
                mm.then_inc(qkv_done, 1)

            def transposes(n):
                pe.wait_ge(x2_made, n + 1)
                pe.wait_ge(res1_made, n + 1)
                for k in range(DK):
                    for t in range(TT):
                        mm = nc.tensor.transpose(x2T_ps[k][:, t * P:(t + 1) * P], x2[:, t, k * P:(k + 1) * P], ident[:, :])
                mm.then_inc(tr_done, 1)

            def chunk(n, first=False, last=False):
                pe.wait_ge(elu_made, n + 1)
                if not first:
                    pe.wait_ge(den_step, 2 * n - 1)
                for t in range(TT):
                    nc.tensor.matmul(s_ps[:, t, :], kT[:, t * P:(t + 1) * P], qT[:, t * P:(t + 1) * P], start=True, stop=True)
                for t in range(TT):
                    mm = nc.tensor.matmul(delta_ps[:, t, :], kv1[:, t, 0:KH], kv1[:, t, KH:2 * KH + 1], start=True, stop=True)
                mm.then_inc(sd_done, 1)
                pe.wait_ge(ctx_copied, n + 1)
                if not first:
                    pe.wait_ge(u_copied, n)
                for t in range(TT):
                    for k in range(DK):
                        mm = nc.tensor.matmul(u_ps[:, t, :], ctx_chunk[:, k, t * P:(t + 1) * P], wvo[:, k, :],
                                              start=(k == 0), stop=(k == DK - 1))
                mm.then_inc(u_done, 1)
                pe.wait_ge(sT_made, n + 1)
                pe.wait_ge(state_step, (TT + 1) * (n + 1))
                for t in range(TT):
                    cols = slice(t * P, (t + 1) * P)
                    nc.tensor.matmul(numT_ps[:, cols], kv1[:, t, KH:2 * KH + 1], sT[:, t, :], start=True, stop=False)
                    mm = nc.tensor.matmul(numT_ps[:, cols], state[:, t, :], qT[:, cols], start=False, stop=True)
                mm.then_inc(num_done, 1)
                if not first:
                    transposes(n - 1)
                if not last:
                    qkv(n + 1)
                pe.wait_ge(num_copied, n + 1)
                if not first:
                    pe.wait_ge(x2T_copied, n)
                for t in range(TT):
                    cols = slice(t * P, (t + 1) * P)
                    nc.tensor.matmul(y_ps[:, t, :], numT[0:KH, cols], wo[:, :], start=True, stop=True)
                for t in range(TT):
                    cols = slice(t * P, (t + 1) * P)
                    mm = nc.tensor.matmul(den_ps[:, t:t + 1], numT[:, cols], den_pick[:, :], start=True, stop=True)
                mm.then_inc(y_done, 1)

            pe.wait_ge(got_wqkv, 16)
            qkv(0)
            pe.wait_ge(got_wv, 16)
            pe.wait_ge(got_wout, 16)
            for c in range(DK):
                for k in range(IK):
                    mm = nc.tensor.matmul(wvo_ps[c], wv[:, k, c * P:(c + 1) * P], wout[:, k, :],
                                          start=(k == 0), stop=(k == IK - 1))
            mm.then_inc(wvo_done, 1)
            pe.wait_ge(wvo_copied, 1)
            pe.wait_ge(dve_consts, 1)
            pe.wait_ge(ident_made, 1)
            pe.wait_ge(got_wo, 16)
            chunk(0, first=True)
            with pe.Fori(1, CHUNKS - 1) as n:
                chunk(n)
            chunk(CHUNKS - 1, last=True)
            transposes(CHUNKS - 1)
            pe.wait_ge(flag_step, 1)
            nc.tensor.matmul(flag_ps, unequal_sum[:, :], ones[:, :], start=True, stop=True).then_inc(flag_sum, 1)
            pe.wait_ge(flag_made, 1)
            finer = pe.value_load(flag[0:1, 0:1], min_val=0, max_val=1)

            def ffn(n, finer):
                def bank(slot, b):
                    return ps[:, 2 * (slot % 2) + b, :]

                def pair_free(slot):
                    if slot < 2:
                        pe.wait_ge(out_read, OUT_SLOTS * n + slot + 1)
                    elif slot - 2 < GATE_SLOTS:
                        pe.wait_ge(gate_made, GATE_SLOTS * n + slot - 1)
                    else:
                        pe.wait_ge(gelu_made, 2 * FK * n + 2 * (slot - 1 - GATE_SLOTS))

                piece = 0
                pe.wait_ge(xs_ready, n + 1)
                for m in range(GATE_SLOTS):
                    pair_free(m)
                    if finer:
                        pe.wait_ge(lo_made, LO_PIECES * n + piece + 1)
                        piece += 1
                        for b in range(2):
                            for k in range(DK):
                                c = (DK * b + k) * P
                                for part in range(2):
                                    mm = nc.tensor.matmul(bank(m, b), w_lo[:, c:c + P], xs[part][:, k, :],
                                                          start=(k == 0 and part == 0), stop=False)
                        mm.then_inc(lo_used, 1)
                    for b, w in enumerate((W1, W2)):
                        for k in range(DK):
                            c = w + k * F + m * P
                            for part in range(2):
                                mm = nc.tensor.matmul(bank(m, b), W[:, c:c + P], xs[part][:, k, :],
                                                      start=(k == 0 and part == 0 and not finer),
                                                      stop=(k == DK - 1 and part == 1))
                    mm.then_inc(slot_done, 1)

                for layer, (w, h) in enumerate(((H1, h1), (H2, h2))):
                    for j in range(HID_SLOTS):
                        slot = GATE_SLOTS + layer * HID_SLOTS + j
                        pair_free(slot)
                        if finer:
                            pe.wait_ge(h_ready, TILES * n + (layer + 1) * FK)
                            for b in range(2):
                                for k0 in (0, FK // 2):
                                    pe.wait_ge(lo_made, LO_PIECES * n + piece + 1)
                                    piece += 1
                                    for k in range(FK // 2):
                                        for part in range(2):
                                            mm = nc.tensor.matmul(bank(slot, b), w_lo[:, k * P:(k + 1) * P],
                                                                  h[part][:, k0 + k, :],
                                                                  start=(k0 + k == 0 and part == 0), stop=False)
                                    mm.then_inc(lo_used, 1)
                        for k in range(FK):
                            if j == 0:
                                pe.wait_ge(h_ready, TILES * n + layer * FK + k + 1)
                            for b in range(2):
                                c = w + k * F + (2 * j + b) * P
                                for part in range(2):
                                    mm = nc.tensor.matmul(bank(slot, b), W[:, c:c + P], h[part][:, k, :],
                                                          start=(k == 0 and part == 0 and not finer),
                                                          stop=(k == FK - 1 and part == 1))
                        mm.then_inc(slot_done, 1)

                for pair in range(OUT_SLOTS):
                    slot = SLOTS - OUT_SLOTS + pair
                    pair_free(slot)
                    if finer:
                        pe.wait_ge(h_ready, TILES * (n + 1))
                        for k0 in range(0, FK, 2):
                            pe.wait_ge(lo_made, LO_PIECES * n + piece + 1)
                            piece += 1
                            for b in range(2):
                                t = 2 * pair + b
                                for k in range(2):
                                    for part in range(2):
                                        mm = nc.tensor.matmul(bank(slot, b)[:, 0:D], h1[part][:, k0 + k, t * P:(t + 1) * P],
                                                              w_lo[:, k * D:(k + 1) * D],
                                                              start=(k0 + k == 0 and part == 0), stop=False)
                            mm.then_inc(lo_used, 1)
                    for k in range(FK):
                        if pair == 0:
                            pe.wait_ge(h_ready, TILES * n + 2 * FK + k + 1)
                        for b in range(2):
                            t = 2 * pair + b
                            for part in range(2):
                                mm = nc.tensor.matmul(bank(slot, b)[:, 0:D], h1[part][:, k, t * P:(t + 1) * P],
                                                      W[:, W3 + k * D:W3 + (k + 1) * D],
                                                      start=(k == 0 and part == 0 and not finer),
                                                      stop=(k == FK - 1 and part == 1))
                    mm.then_inc(slot_done, 1)

            with pe.If(finer > 0):
                with pe.Fori(0, CHUNKS) as n:
                    ffn(n, True)
            with pe.Else():
                with pe.Fori(0, CHUNKS) as n:
                    ffn(n, False)


_IN = ["x_tok", "x_feat", "ctx_feat", "wqkv", "wo", "wv", "wout", "bout", "ffn_w", "scales", "w3s"]


def kernel(x, ctx_1024, L0_attn_Wq, L0_attn_Wk, L0_attn_Wv, L0_attn_Wo, L0_xattn_Wq, L0_xattn_Wkv, L0_xattn_Wout,
           L0_xattn_bout, L0_ffn_w1_w, L0_ffn_w1_s, L0_ffn_w2_w, L0_ffn_w2_s, L0_ffn_h1_w, L0_ffn_h1_s, L0_ffn_h2_w,
           L0_ffn_h2_s, L0_ffn_w3_w, L0_ffn_w3_s):
    import numpy as np
    import concourse.bacc as bacc
    from concourse.bass_utils import run_bass_kernel_spmd

    def features_on_partitions(a):
        a = np.asarray(a)
        return a.reshape(-1, P, a.shape[1]).transpose(1, 0, 2)

    x0 = np.asarray(x)[0]
    wkv = np.asarray(L0_xattn_Wkv)
    ffn = [L0_ffn_w1_w, L0_ffn_w2_w, L0_ffn_h1_w, L0_ffn_h2_w, L0_ffn_w3_w]
    arrays = {
        "x_tok": x0.reshape(CHUNKS, TT, P, D).transpose(0, 2, 1, 3),
        "x_feat": x0.T.reshape(DK, P, CHUNKS, T).transpose(2, 1, 0, 3),
        "ctx_feat": features_on_partitions(np.asarray(ctx_1024)[0].T),
        "wqkv": features_on_partitions(np.concatenate([np.asarray(w).T for w in (L0_attn_Wq, L0_attn_Wk, L0_attn_Wv)], axis=1)),
        "wo": np.asarray(L0_attn_Wo).T,
        "wv": features_on_partitions(wkv[:, INNER:].T),
        "wout": features_on_partitions(L0_xattn_Wout),
        "bout": np.asarray(L0_xattn_bout),
        "ffn_w": np.concatenate([features_on_partitions(np.asarray(w).T).reshape(P, -1) for w in ffn], axis=1),
        "scales": np.concatenate([np.asarray(s).reshape(FK, P).T for s in (L0_ffn_w1_s, L0_ffn_w2_s, L0_ffn_h1_s, L0_ffn_h2_s)], axis=1),
        "w3s": np.asarray(L0_ffn_w3_s),
    }
    arrays = {name: np.ascontiguousarray(a) for name, a in arrays.items()}
    nc = bacc.Bacc("TRN2", target_bir_lowering=False, num_devices=1)
    args = [nc.dram_tensor("in_" + name, arrays[name].shape, mybir.dt.from_np(arrays[name].dtype), kind="ExternalInput").ap() for name in _IN]
    out = nc.dram_tensor("layer_out", (CHUNKS, P, TT * D), F32, kind="ExternalOutput").ap()
    decoder_layer(nc, *args, out)
    r = run_bass_kernel_spmd(nc, [{"in_" + name: a for name, a in arrays.items()}], core_ids=[0])
    got = r.results[0]["layer_out"]
    return got.reshape(CHUNKS, P, TT, D).transpose(0, 2, 1, 3).reshape(1, S, D)
```

```python
from contextlib import ExitStack

import concourse.bass as bass
from concourse import mybir

ALU = mybir.AluOpType
ACT = mybir.ActivationFunctionType
AX = mybir.AxisListType
F32 = mybir.dt.float32
F32R = mybir.dt.float32r
I32 = mybir.dt.int32

P = 128
S = 2048
SC = 1601
D = 256
DK = D // P
KH = 64
INNER = 1024
IK = INNER // P
F = 1024
FK = F // P
T = 512
CHUNKS = S // T
MEAN_TILE = -(-SC // P)
TT = T // P
LAST_CTX = MEAN_TILE + 1 - (CHUNKS - 1) * TT
LAST_KEYS = SC - (CHUNKS - 1) * T
assert 0 < LAST_CTX <= TT
EPS = 1e-5
DEN_EPS = 1e-6

W1, W2, H1, H2, W3 = 0, DK * F, 2 * DK * F, 2 * DK * F + FK * F, 2 * DK * F + 2 * FK * F
WCOLS = W3 + FK * D
EARLY = 2 * CHUNKS
ECOLS = H2 // EARLY
LATE = 10
LCOLS = (WCOLS - H2) // LATE
assert ECOLS * EARLY == H2 and LCOLS * LATE == WCOLS - H2
PIECES = EARLY + LATE

PAIRS = 3
GATE_SLOTS = FK
HID_SLOTS = FK // 2
OUT_SLOTS = TT // 2
SLOTS = GATE_SLOTS + 2 * HID_SLOTS + OUT_SLOTS
TILES = 3 * FK
HF = 3
STORES = CHUNKS + 1
LO_PIECES = GATE_SLOTS + 2 * HID_SLOTS * 4 + OUT_SLOTS * 4
assert SLOTS % PAIRS == 0 and TILES % HF == 0 and LCOLS == F


def decoder_layer(nc, x_tok, x_feat, ctx_feat, wqkv_d, wo_d, wv_d, wout_d, bout_d, ffn_w, scales_d, w3s_d, out):
    with ExitStack() as ctx:
        def sem(name):
            return ctx.enter_context(nc.semaphore(name))

        def keep(name, shape, dt=F32):
            return ctx.enter_context(nc.sbuf_tensor(name, shape, dt))

        W = keep("W", [P, WCOLS], F32R)
        x2_all = keep("x2_all", [P, CHUNKS, TT * D])
        x2T_all = keep("x2T_all", [P, DK, S])
        scales = keep("scales", [P, 4 * FK])
        w3s = keep("w3s", [P, D])
        stats = keep("stats", [P, TT, 6])
        mv = keep("mv", [P, TT, 2])
        veps = keep("veps", [P, TT])
        rstd = keep("rstd", [P, TT])
        eps = keep("eps", [P, TT])
        minus_half = keep("minus_half", [P, TT])
        unequal = keep("unequal", [P, PIECES])
        unequal_sum = keep("unequal_sum", [P, 1])
        ones = keep("ones", [P, 1])
        flag = keep("flag", [1, 1], I32)

        def area(stack):
            return lambda name, shape, dt=F32: stack.enter_context(nc.sbuf_tensor(name, shape, dt))

        with ExitStack() as attention:
            with ExitStack() as low:
                sb = area(low)
                ctx_chunk = sb("ctx_chunk", [P, DK, T])
                e_qk = sb("e_qk", [P, T])
                r_qk = sb("r_qk", [P, T])
                xT = sb("xT", [P, DK, T])
                e_k = sb("e_k", [P, TT, KH])
                r_k = sb("r_k", [P, TT, KH])
                xt = sb("xt", [P, TT, D])
                wqkv = sb("wqkv", [P, DK, 3 * KH])
                wo = sb("wo", [KH, D])
                wvo = sb("wvo", [P, DK, D])
                mask = sb("mask", [P, TT, P])
                qT = sb("qT", [KH, T])
                kT = sb("kT", [KH, T])
                kv1 = sb("kv1", [P, TT, 2 * KH + 1])
                sT = sb("sT", [P, TT, P])
                state = sb("state", [KH, TT + 1, KH + 1])
                numT = sb("numT", [KH + 1, T])
                den = sb("den", [P, TT])
                rden = sb("rden", [P, TT])
                den_pick = sb("den_pick", [KH + 1, 1])
                ctx_sums = sb("ctx_sums", [P, DK, CHUNKS])
                ctx_sum = sb("ctx_sum", [P, DK])
                ctx_mean = sb("ctx_mean", [P, DK])
            sb = area(attention)
            sb("below_h2", [P, 2 * DK * T + HF * T + 2 * T + TT * D + 2 * FK * T])
            with ExitStack() as early:
                wv = area(early)("wv", [P, IK, D])
                wout = area(early)("wout", [P, IK, D])
            res1 = sb("res1", [P, TT, D])
            ub = sb("ub", [P, TT, D])
            res2 = sb("res2", [P, TT, D])
            x2 = sb("x2", [P, TT, D])
            stage = [sb(f"stage{i}", [P, ECOLS]) for i in range(2)]
            bout = sb("bout", [P, D])
            ident = sb("ident", [P, P])

        with ExitStack() as feed_forward:
            sb = area(feed_forward)
            xs = [sb(f"xs_{p}", [P, DK, T], F32R) for p in ("hi", "lo")]
            hf = [sb(f"hf{i}", [P, T]) for i in range(HF)]
            with ExitStack() as first_chunk:
                late_stage = [area(first_chunk)(f"late_stage{i}", [P, LCOLS]) for i in range(2)]
            w_again = sb("w_again", [P, T])
            w_lo = sb("w_lo", [P, T], F32R)
            fin = sb("fin", [P, TT, D])
            h1 = [sb(f"h1_{p}", [P, FK, T], F32R) for p in ("hi", "lo")]
            h2 = [sb(f"h2_{p}", [P, FK, T], F32R) for p in ("hi", "lo")]

        ps = ctx.enter_context(nc.psum_tensor("ps", [P, 8, 512], F32))
        QK, KV, SC_B, Y_B, ND_B, U_B = 0, 1, 2, 3, 5, 6
        kv_ps = ps[:, KV, :].rearrange("p (t c) -> p t c", t=TT)
        s_ps = ps[:, SC_B, :].rearrange("p (t c) -> p t c", t=TT)
        y_ps = ps[:, Y_B:Y_B + 2, :].rearrange("p b (t c) -> p (b t) c", t=2)
        u_ps = ps[:, U_B:U_B + 2, :].rearrange("p b (t c) -> p (b t) c", t=2)
        delta_ps = ps[0:KH, ND_B, 0:TT * (KH + 1)].rearrange("p (t c) -> p t c", t=TT)
        numT_ps = ps[0:KH + 1, ND_B, :]
        den_ps = ps[:, ND_B, 0:TT]
        wvo_ps = [ps[:, U_B + c, 0:D] for c in range(DK)]
        x2T_ps = [ps[:, U_B + c, :] for c in range(DK)]
        flag_ps = ps[0:1, U_B, 0:1]

        got_xT, got_xt, got_wqkv, got_wo = sem("got_xT"), sem("got_xt"), sem("got_wqkv"), sem("got_wo")
        got_wv, got_wout, got_ctx, got_bout = sem("got_wv"), sem("got_wout"), sem("got_ctx"), sem("got_bout")
        got_scales, got_w3s = sem("got_scales"), sem("got_w3s")
        got_stage = [sem("got_stage0"), sem("got_stage1")]
        got_late = [sem("got_late0"), sem("got_late1")]
        got_again, stored = sem("got_again"), sem("stored")
        ident_zero, ident_made = sem("ident_zero"), sem("ident_made")
        mask_one, mask_made = sem("mask_one"), sem("mask_made")
        dve_consts, pool_consts = sem("dve_consts"), sem("pool_consts")
        wvo_done, qkv_done, sd_done, u_done = sem("wvo_done"), sem("qkv_done"), sem("sd_done"), sem("u_done")
        num_done, y_done, tr_done, flag_sum = sem("num_done"), sem("y_done"), sem("tr_done"), sem("flag_sum")
        wvo_copied, qkv_acted, u_copied = sem("wvo_copied"), sem("qkv_acted"), sem("u_copied")
        num_copied, x2T_copied, w_rounded = sem("num_copied"), sem("x2T_copied"), sem("w_rounded")
        x2_kept = sem("x2_kept")
        ctx_summed, mean_step, tail_filled = sem("ctx_summed"), sem("mean_step"), sem("tail_filled")
        sT_made, state_step, elu_made = sem("sT_made"), sem("state_step"), sem("elu_made")
        den_step, res1_made, res2_made = sem("den_step"), sem("res1_made"), sem("res2_made")
        stats1_made, mv1_made, x1_made = sem("stats1_made"), sem("mv1_made"), sem("x1_made")
        stats2_made, mv2_made, x2_made = sem("stats2_made"), sem("mv2_made"), sem("x2_made")
        w_looked, weights_looked, flag_made = sem("w_looked"), sem("weights_looked"), sem("flag_made")
        ub_made = sem("ub_made")
        veps_made, rstd_made = sem("veps_made"), sem("rstd_made")
        slot_done = sem("slot_done")
        xs_hi_made, xs_ready = sem("xs_hi_made"), sem("xs_ready")
        silu_made, gate_made = sem("silu_made"), sem("gate_made")
        gelu_made = sem("gelu_made")
        hi_made, h_ready = sem("hi_made"), sem("h_ready")
        out_read = sem("out_read")
        out_added, stats3_made, mv3_made, out_made = sem("out_added"), sem("stats3_made"), sem("mv3_made"), sem("out_made")
        lo_made, lo_used = sem("lo_made"), sem("lo_used")

        block = ctx.enter_context(nc.Block())


        @block.sync
        def _(sp):
            sp.dma_start(xT[:, :, :], x_feat[0]).then_inc(got_xT, 16)
            sp.dma_start(wv[:, :, :], wv_d).then_inc(got_wv, 16)
            sp.dma_start(wout[:, :, :], wout_d).then_inc(got_wout, 16)

            def load_piece(n, i):
                sp.dma_start(stage[i][:, :], ffn_w[:, bass.ds((2 * n + i) * ECOLS, ECOLS)]).then_inc(got_stage[i], 16)

            def load_xT(n):
                sp.wait_ge(qkv_done, n)
                sp.dma_start(xT[:, :, :], x_feat[bass.ds(n, 1)].rearrange("a p k t -> (a p) k t")).then_inc(got_xT, 16)

            def load_ctx(n, cols=T):
                sp.wait_ge(u_done, n)
                sp.wait_ge(ctx_summed, n)
                sp.dma_start(ctx_chunk[:, :, 0:cols], ctx_feat[:, :, bass.ds(n * T, cols)]).then_inc(got_ctx, 16)

            load_piece(0, 0)
            load_xT(1)
            load_piece(0, 1)
            load_ctx(1)

            def next_loads(n, ctx_cols=T, last=False):
                sp.wait_ge(w_looked, 2 * n + 1)
                load_piece(n + 1, 0)
                if not last:
                    load_xT(n + 2)
                sp.wait_ge(res1_made, n + 1)
                sp.dma_start(xt[:, :, :], x_tok[bass.ds(n + 1, 1)].rearrange("a p t d -> (a p) t d")).then_inc(got_xt, 16)
                if not last:
                    load_ctx(n + 2, ctx_cols)
                sp.wait_ge(w_looked, 2 * n + 2)
                load_piece(n + 1, 1)

            with sp.Fori(0, CHUNKS - 3) as n:
                next_loads(n)
            next_loads(CHUNKS - 3, ctx_cols=LAST_KEYS)
            next_loads(CHUNKS - 2, last=True)

            sp.wait_ge(res1_made, CHUNKS)
            for i in range(LATE):
                if i >= 2:
                    sp.wait_ge(w_looked, EARLY + i - 1)
                c = H2 + i * LCOLS
                sp.dma_start(late_stage[i % 2][:, :], ffn_w[:, c:c + LCOLS]).then_inc(got_late[i % 2], 16)

            def store(n, made, c0, c1):
                sp.wait_ge(out_made, made)
                sp.dma_start(out[bass.ds(n, 1), :, c0:c1].rearrange("a p c -> (a p) c"),
                             fin[:, c0 // D:c1 // D, :].rearrange("p t d -> p (t d)")).then_inc(stored, 16)

            def stores_of_last(made):
                store(CHUNKS - 1, made, 0, 2 * D)
                store(CHUNKS - 1, made + 1, 2 * D, TT * D)

            with sp.Fori(0, CHUNKS - 1) as n:
                store(n, n + 1, 0, TT * D)
            stores_of_last(CHUNKS)

            gates = ffn_w[:, W1:H1].rearrange("p (k o) -> p k o", o=F)
            hidden = [ffn_w[:, h:h + FK * F].rearrange("p (k o) -> p k o", o=F) for h in (H1, H2)]

            def lo_pieces():
                for m in range(GATE_SLOTS):
                    yield gates[:, :, m * P:(m + 1) * P]
                for w in hidden:
                    for m in range(FK):
                        for k in (0, FK // 2):
                            yield w[:, k:k + FK // 2, m * P:(m + 1) * P]
                for _ in range(OUT_SLOTS):
                    for k in range(0, FK, 2):
                        yield ffn_w[:, W3 + k * D:W3 + (k + 2) * D]

            def load_again(n):
                for i, piece in enumerate(lo_pieces()):
                    if i or n is not CHUNKS:
                        sp.wait_ge(lo_made, LO_PIECES * (n - CHUNKS) + i)
                    dst = w_again[:, :]
                    if len(piece.shape) == 3:
                        dst = dst.rearrange("p (k o) -> p k o", o=P)
                    sp.dma_start(dst, piece).then_inc(got_again, 16)
                    if i == GATE_SLOTS + HID_SLOTS * 4 and n is not CHUNKS:
                        store(n - 1 - CHUNKS, n + 1, 0, TT * D)

            sp.wait_ge(flag_made, 1)
            finer = sp.value_load(flag[0:1, 0:1], min_val=0, max_val=1)
            with sp.If(finer > 0):
                sp.wait_ge(stored, 16 * STORES)
                load_again(CHUNKS)
                with sp.Fori(CHUNKS + 1, 2 * CHUNKS) as n:
                    load_again(n)
                stores_of_last(2 * CHUNKS + 1)
                sp.wait_ge(stored, 2 * 16 * STORES)
            with sp.Else():
                sp.wait_ge(stored, 16 * STORES)

        @block.gpsimd
        def _(pool):
            nc.gpsimd.memset(ident[:, :], 0.0).then_inc(ident_zero, 1)
            nc.gpsimd.memset(mask[:, :, :], 1.0).then_inc(mask_one, 1)
            nc.gpsimd.memset(eps[:, :], EPS)
            nc.gpsimd.memset(minus_half[:, :], -0.5).then_inc(pool_consts, 1)
            pool.wait_ge(ident_zero, 1)
            nc.gpsimd.affine_select(out=ident[:, :], in_=ident[:, :], compare_op=ALU.not_equal, fill=1.0,
                                    base=0, pattern=[[-1, P]], channel_multiplier=1).then_inc(ident_made, 1)
            pool.wait_ge(mask_one, 1)
            nc.gpsimd.affine_select(out=mask[:, :, :], in_=mask[:, :, :], compare_op=ALU.is_ge, fill=0.0,
                                    base=0, pattern=[[0, TT], [1, P]], channel_multiplier=-1).then_inc(mask_made, 1)
            pool.wait_ge(pool_consts, 1)

            def inverse_root(count, mv_made, at_least, c0, c1):
                pool.wait_ge(mv_made, at_least)
                nc.gpsimd.tensor_tensor(veps[:, c0:c1], mv[:, c0:c1, 1], eps[:, c0:c1], ALU.add).then_inc(veps_made, 1)
                pool.wait_ge(veps_made, count)
                nc.gpsimd.tensor_tensor(rstd[:, c0:c1], veps[:, c0:c1], minus_half[:, c0:c1], ALU.pow).then_inc(rstd_made, 1)

            def chunk(n, first=False):
                if not first:
                    inverse_root(2 * n, mv2_made, n, 0, TT)
                pool.wait_ge(u_copied, n + 1)
                nc.gpsimd.tensor_tensor(ub[:, :, :], ub[:, :, :], bout[:, :].unsqueeze(1).to_broadcast([P, TT, D]),
                                        ALU.add).then_inc(ub_made, 1)
                inverse_root(2 * n + 1, mv1_made, n + 1, 0, TT)

            pool.wait_ge(got_bout, 16)
            chunk(0, first=True)
            with pool.Fori(1, CHUNKS) as n:
                chunk(n)
            inverse_root(2 * CHUNKS, mv2_made, CHUNKS, 0, TT)

            def third_norms(done):
                with pool.Fori(0, CHUNKS - 1) as n:
                    inverse_root(2 * CHUNKS + done + n + 1, mv3_made, done + n + 1, 0, TT)
                for half in range(2):
                    count = done + CHUNKS + half
                    inverse_root(2 * CHUNKS + count, mv3_made, count, 2 * half, 2 * half + 2)

            third_norms(0)
            pool.wait_ge(flag_made, 1)
            finer = pool.value_load(flag[0:1, 0:1], min_val=0, max_val=1)
            with pool.If(finer > 0):
                third_norms(STORES)

        @block.scalar
        def _(act):
            act.sem_inc(x2T_copied, 1)
            act.sem_inc(x2_kept, 1)
            act.dma_start(wqkv[:, :, :], wqkv_d).then_inc(got_wqkv, 16)
            act.dma_start(wo[:, :], wo_d).then_inc(got_wo, 16)
            act.dma_start(bout[:, :], bout_d.partition_broadcast(P)).then_inc(got_bout, 16)
            act.dma_start(w3s[:, :], w3s_d.partition_broadcast(P)).then_inc(got_w3s, 16)
            act.dma_start(scales[:, :], scales_d).then_inc(got_scales, 16)
            act.dma_start(ctx_chunk[:, :, :], ctx_feat[:, :, 0:T]).then_inc(got_ctx, 16)
            act.dma_start(xt[:, :, :], x_tok[0]).then_inc(got_xt, 16)

            def qkv_parts(m):
                act.wait_ge(qkv_done, m + 1)
                nc.scalar.activation(e_qk[:, :], ps[:, QK, :], ACT.Exp)
                nc.scalar.activation(r_qk[:, :], ps[:, QK, :], ACT.Relu)
                nc.scalar.activation(e_k[:, :, :], kv_ps[:, :, 0:KH], ACT.Exp)
                nc.scalar.activation(r_k[:, :, :], kv_ps[:, :, 0:KH], ACT.Relu)
                nc.scalar.copy(kv1[:, :, KH:2 * KH], kv_ps[:, :, KH:2 * KH]).then_inc(qkv_acted, 1)

            def round_piece(n, i):
                act.wait_ge(got_stage[i], 16 * (n + 1))
                nc.scalar.copy(W[:, bass.ds((2 * n + i) * ECOLS, ECOLS)], stage[i][:, :]).then_inc(w_rounded, 1)

            def round_late(i):
                act.wait_ge(got_late[i % 2], 16 * (i // 2 + 1))
                c = H2 + i * LCOLS
                nc.scalar.copy(W[:, c:c + LCOLS], late_stage[i % 2][:, :]).then_inc(w_rounded, 1)

            def keep_x2(n):
                act.wait_ge(x2_made, n + 1)
                nc.scalar.copy(x2_all[:, bass.ds(n, 1), :].rearrange("p a c -> p (a c)"),
                               x2[:, :, :].rearrange("p t d -> p (t d)")).then_inc(x2_kept, 1)

            def keep_x2T(n):
                act.wait_ge(tr_done, n + 2)
                for k in range(DK):
                    c = nc.scalar.copy(x2T_all[:, k, bass.ds(n * T, T)], x2T_ps[k])
                c.then_inc(x2T_copied, 1)

            def chunk(n, first=False, last=False):
                act.wait_ge(num_done, n + 1)
                nc.scalar.copy(numT[:, :], numT_ps).then_inc(num_copied, 1)
                round_piece(n, 0)
                act.wait_ge(u_done, n + 1)
                if not first:
                    act.wait_ge(res2_made, n)
                if not last:
                    nc.scalar.copy(ub[:, :, :], u_ps).then_inc(u_copied, 1)
                else:
                    nc.scalar.copy(ub[:, 0:LAST_CTX, :], u_ps[:, 0:LAST_CTX, :])
                    mean_u = u_ps[:, LAST_CTX - 1, :].unsqueeze(1).to_broadcast([P, TT - LAST_CTX, D])
                    nc.scalar.copy(ub[:, LAST_CTX:TT, :], mean_u).then_inc(u_copied, 1)
                if not last:
                    act.wait_ge(elu_made, n + 1)
                    qkv_parts(n + 1)
                else:
                    act.wait_ge(x2T_copied, 2)
                    split_x_hi(0)
                if not first:
                    keep_x2(n - 1)
                    keep_x2T(n - 1)
                round_piece(n, 1)

            def split_x_hi(n):
                nc.scalar.copy(xs[0][:, :, :], x2T_all[:, :, bass.ds(n * T, T)]).then_inc(xs_hi_made, 1)

            qkv_parts(0)
            act.wait_ge(wvo_done, 1)
            for c in range(DK):
                cp = nc.scalar.copy(wvo[:, c, :], wvo_ps[c])
            cp.then_inc(wvo_copied, 1)
            chunk(0, first=True)
            with act.Fori(1, CHUNKS - 1) as n:
                chunk(n)
            chunk(CHUNKS - 1, last=True)

            def hi(n, tile):
                h = h1 if tile // FK != 1 else h2
                nc.scalar.copy(h[0][:, tile % FK, :], hf[tile % HF][:, :]).then_inc(hi_made, 1)

            def ffn(n, base=0, first=False, last=False):
                for m in range(GATE_SLOTS + 1):
                    if m < GATE_SLOTS:
                        act.wait_ge(slot_done, SLOTS * n + m + 1)
                        if m >= HF:
                            act.wait_ge(h_ready, TILES * n + m - HF + 1)
                        nc.scalar.activation(hf[m % HF][:, :], ps[:, 2 * (m % PAIRS), :], ACT.Silu,
                                             scale=scales[:, m:m + 1]).then_inc(silu_made, 1)
                    if m:
                        act.wait_ge(gate_made, GATE_SLOTS * n + m)
                        hi(n, m - 1)
                for layer in range(2):
                    if layer == 1 and not last:
                        act.wait_ge(slot_done, SLOTS * n + GATE_SLOTS)
                        split_x_hi(n + 1 - base)
                    for j in range(HID_SLOTS):
                        slot = GATE_SLOTS + layer * HID_SLOTS + j
                        act.wait_ge(slot_done, SLOTS * n + slot + 1)
                        for b in range(2):
                            tile = FK * (layer + 1) + 2 * j + b
                            act.wait_ge(h_ready, TILES * n + tile - HF + 1)
                            s = FK * (layer + 2) + 2 * j + b
                            nc.scalar.activation(hf[tile % HF][:, :], ps[:, 2 * (slot % PAIRS) + b, :], ACT.Gelu,
                                                 scale=scales[:, s:s + 1]).then_inc(gelu_made, 1)
                        if first and layer == 0 and j == 0:
                            act.wait_ge(res2_made, CHUNKS)
                        for b in range(2):
                            tile = FK * (layer + 1) + 2 * j + b
                            act.wait_ge(gelu_made, 2 * FK * n + tile - FK + 1)
                            hi(n, tile)
                        if first and layer == 0:
                            round_late(2 * j)
                            round_late(2 * j + 1)
                            if j == 1:
                                keep_x2(CHUNKS - 1)
                                keep_x2T(CHUNKS - 1)
                        if first and layer == 1 and j < 2:
                            round_late(2 * HID_SLOTS + j)

            act.wait_ge(got_scales, 16)
            ffn(0, first=True)
            with act.Fori(1, CHUNKS - 1) as n:
                ffn(n)
            ffn(CHUNKS - 1, last=True)

            act.wait_ge(flag_made, 1)
            finer = act.value_load(flag[0:1, 0:1], min_val=0, max_val=1)
            with act.If(finer > 0):
                split_x_hi(0)
                with act.Fori(CHUNKS, 2 * CHUNKS - 1) as n:
                    ffn(n, base=CHUNKS)
                ffn(2 * CHUNKS - 1, base=CHUNKS, last=True)

        @block.vector
        def _(dve):
            nc.vector.memset(den_pick[0:KH, :], 0.0)
            nc.vector.memset(den_pick[KH:KH + 1, :], 1.0)
            nc.vector.memset(ones[:, :], 1.0)
            nc.vector.memset(kv1[:, :, 2 * KH:2 * KH + 1], 1.0).then_inc(dve_consts, 1)

            def elu(m):
                dve.wait_ge(qkv_acted, m + 1)
                nc.vector.scalar_tensor_tensor(qT[:, :], e_qk[0:KH, :], 1.0, r_qk[0:KH, :], ALU.min, ALU.add)
                nc.vector.scalar_tensor_tensor(kT[:, :], e_qk[KH:P, :], 1.0, r_qk[KH:P, :], ALU.min, ALU.add)
                nc.vector.scalar_tensor_tensor(kv1[:, :, 0:KH], e_k[:, :, :], 1.0, r_k[:, :, :],
                                               ALU.min, ALU.add).then_inc(elu_made, 1)

            def look(g, source, c, cols):
                dve.wait_ge(w_rounded, g + 1)
                nc.vector.scalar_tensor_tensor(source[:, :], source[:, :], 1.0, W[:, bass.ds(c, cols)].bitcast(F32),
                                               ALU.mult, ALU.not_equal,
                                               accum_out=unequal[:, bass.ds(g, 1)]).then_inc(w_looked, 1)

            def look_early(n, i):
                look(2 * n + i, stage[i], (2 * n + i) * ECOLS, ECOLS)

            def look_late(i):
                look(EARLY + i, late_stage[i % 2], H2 + i * LCOLS, LCOLS)

            def moments(src, at_least, made, stats_made, mv_made, count):
                dve.wait_ge(made, at_least)
                for t in range(TT):
                    s = nc.vector.bn_stats(stats[:, t, :], src[:, t, :])
                s.then_inc(stats_made, 1)
                dve.wait_ge(dve_consts, 1)
                dve.wait_ge(stats_made, count)
                for t in range(TT):
                    s = nc.vector.bn_aggr(mv[:, t, :], stats[:, t, :])
                s.then_inc(mv_made, 1)

            def norm(dst, src, made):
                for t in range(TT):
                    s = nc.vector.tensor_scalar(dst[:, t, :], src[:, t, :], mv[:, t, 0:1], rstd[:, t:t + 1],
                                                ALU.subtract, ALU.mult)
                s.then_inc(made, 1)

            def scores(n, first=False):
                dve.wait_ge(sd_done, n + 1)
                nc.vector.tensor_tensor(sT[:, :, :], s_ps, mask[:, :, :], ALU.mult).then_inc(sT_made, 1)
                if not first:
                    dve.wait_ge(state_step, (TT + 1) * n)
                    nc.vector.tensor_copy(state[:, 0, :], state[:, TT, :]).then_inc(state_step, 1)
                else:
                    nc.vector.memset(state[:, 0, :], 0.0).then_inc(state_step, 1)
                for t in range(TT):
                    dve.wait_ge(state_step, (TT + 1) * n + t + 1)
                    nc.vector.tensor_tensor(state[:, t + 1, :], delta_ps[:, t, :], state[:, t, :],
                                            ALU.add).then_inc(state_step, 1)

            def sum_ctx(n, keys=T):
                dve.wait_ge(got_ctx, 16 * (n + 1))
                nc.vector.tensor_reduce(ctx_sums[:, :, bass.ds(n, 1)], ctx_chunk[:, :, 0:keys], axis=AX.X,
                                        op=ALU.add).then_inc(ctx_summed, 1)
                if keys != T:
                    dve.wait_ge(ctx_summed, CHUNKS)
                    nc.vector.tensor_reduce(ctx_sum[:, :], ctx_sums[:, :, :], axis=AX.X, op=ALU.add).then_inc(mean_step, 1)
                    dve.wait_ge(mean_step, 1)
                    nc.vector.tensor_scalar(ctx_mean[:, :], ctx_sum[:, :], 1.0 / SC, None, ALU.mult).then_inc(mean_step, 1)
                    dve.wait_ge(mean_step, 2)
                    rows = LAST_CTX * P - keys
                    for k in range(DK):
                        s = nc.vector.tensor_copy(ctx_chunk[:, k, keys:LAST_CTX * P],
                                                  ctx_mean[:, k:k + 1].to_broadcast([P, rows]))
                    s.then_inc(tail_filled, 1)

            def chunk(n, ctx_keys=T, first=False, last=False):
                if not first:
                    second_norm(n - 1, lambda: look_early(n, 0))
                else:
                    look_early(n, 0)
                if not last:
                    sum_ctx(n + 1, ctx_keys)
                    elu(n + 1)
                else:
                    split_x_lo(0, 0)
                dve.wait_ge(y_done, n + 1)
                nc.vector.tensor_scalar(den[:, :], den_ps, DEN_EPS, None, ALU.add).then_inc(den_step, 1)
                dve.wait_ge(den_step, 2 * n + 1)
                nc.vector.reciprocal(rden[:, :], den[:, :]).then_inc(den_step, 1)
                dve.wait_ge(den_step, 2 * n + 2)
                dve.wait_ge(got_xt, 16 * (n + 1))
                for t in range(TT):
                    s = nc.vector.scalar_tensor_tensor(res1[:, t, :], y_ps[:, t, :], rden[:, t:t + 1], xt[:, t, :],
                                                       ALU.mult, ALU.add)
                s.then_inc(res1_made, 1)
                if not last:
                    scores(n + 1)
                moments(res1, n + 1, res1_made, stats1_made, mv1_made, n + 1)
                look_early(n, 1)
                dve.wait_ge(rstd_made, 2 * n + 1)
                norm(res1, res1, x1_made)

            def second_norm(n, meanwhile=None):
                dve.wait_ge(x1_made, n + 1)
                dve.wait_ge(ub_made, n + 1)
                nc.vector.tensor_tensor(res2[:, :, :], res1[:, :, :], ub[:, :, :], ALU.add).then_inc(res2_made, 1)
                moments(res2, n + 1, res2_made, stats2_made, mv2_made, n + 1)
                if meanwhile:
                    meanwhile()
                dve.wait_ge(rstd_made, 2 * n + 2)
                dve.wait_ge(x2_kept, n + 1)
                dve.wait_ge(tr_done, n + 1)
                norm(x2, res2, x2_made)

            def split_x_lo(n, chunk_of_x):
                dve.wait_ge(xs_hi_made, n + 1)
                nc.vector.tensor_tensor(xs[1][:, :, :], x2T_all[:, :, bass.ds(chunk_of_x * T, T)],
                                        xs[0][:, :, :].bitcast(F32), ALU.subtract).then_inc(xs_ready, 1)

            elu(0)
            dve.wait_ge(mask_made, 1)
            scores(0, first=True)
            sum_ctx(0)
            chunk(0, first=True)
            with dve.Fori(1, CHUNKS - 2) as n:
                chunk(n)
            chunk(CHUNKS - 2, ctx_keys=LAST_KEYS)
            chunk(CHUNKS - 1, last=True)

            def lo(n, tile):
                h = h1 if tile // FK != 1 else h2
                dve.wait_ge(hi_made, TILES * n + tile + 1)
                nc.vector.tensor_tensor(h[1][:, tile % FK, :], hf[tile % HF][:, :],
                                        h[0][:, tile % FK, :].bitcast(F32), ALU.subtract).then_inc(h_ready, 1)

            gates_w = W[:, W1:H1].rearrange("p (k o) -> p k o", o=F)
            hidden_w = [W[:, h:h + FK * F].rearrange("p (k o) -> p k o", o=F) for h in (H1, H2)]

            def third_norm(n, count, t0, t1, step):
                tiles = range(t0, t1)
                if step == 0:
                    resid = x2_all[:, bass.ds(n, 1), t0 * D:t1 * D].rearrange("p a (t d) -> p (a t) d", d=D)
                    nc.vector.tensor_tensor(fin[:, t0:t1, :], fin[:, t0:t1, :], resid, ALU.add).then_inc(out_added, 1)
                    dve.wait_ge(out_added, count)
                    for t in tiles:
                        s = nc.vector.bn_stats(stats[:, t, :], fin[:, t, :])
                    s.then_inc(stats3_made, 1)
                    dve.wait_ge(dve_consts, 1)
                    dve.wait_ge(stats3_made, count)
                    for t in tiles:
                        s = nc.vector.bn_aggr(mv[:, t, :], stats[:, t, :])
                    s.then_inc(mv3_made, 1)
                else:
                    dve.wait_ge(rstd_made, 2 * CHUNKS + count)
                    for t in tiles:
                        s = nc.vector.tensor_scalar(fin[:, t, :], fin[:, t, :], mv[:, t, 0:1], rstd[:, t:t + 1],
                                                    ALU.subtract, ALU.mult)
                    s.then_inc(out_made, 1)

            def ffn(n, finer=False, first=False, last=False):
                base, extra = (CHUNKS, 1) if finer else (0, 0)

                def weights_lo(i, hi_part):
                    dve.wait_ge(got_again, 16 * (LO_PIECES * (n - base) + i + 1))
                    if i:
                        dve.wait_ge(lo_used, LO_PIECES * (n - base) + i)
                    a, b = w_again[:, :], w_lo[:, :]
                    if len(hi_part.shape) == 3:
                        a, b = (v.rearrange("p (k o) -> p k o", o=P) for v in (a, b))
                    nc.vector.tensor_tensor(b, a, hi_part.bitcast(F32), ALU.subtract).then_inc(lo_made, 1)

                for m in range(GATE_SLOTS + 1):
                    if m < GATE_SLOTS:
                        if finer:
                            weights_lo(m, gates_w[:, :, m * P:(m + 1) * P])
                        dve.wait_ge(silu_made, GATE_SLOTS * n + m + 1)
                        nc.vector.scalar_tensor_tensor(hf[m % HF][:, :], ps[:, 2 * (m % PAIRS) + 1, :],
                                                       scales[:, FK + m:FK + m + 1], hf[m % HF][:, :],
                                                       ALU.mult, ALU.mult).then_inc(gate_made, 1)
                    if m:
                        lo(n, m - 1)
                if first and not finer:
                    second_norm(CHUNKS - 1)
                i = GATE_SLOTS
                for layer in range(2):
                    if layer == 1 and not last:
                        split_x_lo(n + 1, n + 1 - base)
                    for j in range(HID_SLOTS):
                        if finer:
                            for m in (2 * j, 2 * j + 1):
                                for k in (0, FK // 2):
                                    weights_lo(i, hidden_w[layer][:, k:k + FK // 2, m * P:(m + 1) * P])
                                    i += 1
                        for b in range(2):
                            lo(n, FK * (layer + 1) + 2 * j + b)
                        if first and not finer:
                            if layer == 0:
                                look_late(2 * j)
                                look_late(2 * j + 1)
                            elif j < 2:
                                look_late(2 * HID_SLOTS + j)
                        if not first and layer == 0 and j < 2:
                            third_norm(n - 1 - base, n + extra, 0, TT, step=j)
                for pair in range(OUT_SLOTS):
                    if finer:
                        for k in range(0, FK, 2):
                            weights_lo(i, W[:, W3 + k * D:W3 + (k + 2) * D])
                            i += 1
                    slot = SLOTS - OUT_SLOTS + pair
                    bank = 2 * (slot % PAIRS)
                    if pair == 0 and not (first and not finer):
                        dve.wait_ge(stored, 16 * (n + extra))
                    dve.wait_ge(slot_done, SLOTS * n + slot + 1)
                    nc.vector.tensor_tensor(fin[:, 2 * pair:2 * pair + 2, :], ps[:, bank:bank + 2, 0:D],
                                            w3s[:, :].unsqueeze(1).to_broadcast([P, 2, D]), ALU.mult).then_inc(out_read, 1)
                    if last:
                        dve.wait_ge(out_read, OUT_SLOTS * n + pair + 1)
                        for step in range(2):
                            third_norm(n - base, n + extra + pair + 1, 2 * pair, 2 * pair + 2, step)

            dve.wait_ge(got_w3s, 16)
            ffn(0, first=True)
            dve.wait_ge(w_looked, PIECES)
            nc.vector.tensor_reduce(unequal_sum[:, :], unequal[:, :], axis=AX.X, op=ALU.add).then_inc(weights_looked, 1)
            with dve.Fori(1, CHUNKS - 1) as n:
                ffn(n)
            dve.wait_ge(flag_sum, 1)
            nc.vector.tensor_scalar(flag[:, :], flag_ps, 0.0, None, ALU.is_gt).then_inc(flag_made, 1)
            ffn(CHUNKS - 1, last=True)

            dve.wait_ge(flag_made, 1)
            finer = dve.value_load(flag[0:1, 0:1], min_val=0, max_val=1)
            with dve.If(finer > 0):
                split_x_lo(CHUNKS, 0)
                ffn(CHUNKS, finer=True, first=True)
                with dve.Fori(CHUNKS + 1, 2 * CHUNKS - 1) as n:
                    ffn(n, finer=True)
                ffn(2 * CHUNKS - 1, finer=True, last=True)

        @block.tensor
        def _(pe):
            def qkv(m):
                pe.wait_ge(got_xT, 16 * (m + 1))
                for k in range(DK):
                    nc.tensor.matmul(ps[:, QK, :], wqkv[:, k, 0:2 * KH], xT[:, k, :], start=(k == 0), stop=(k == DK - 1))
                for t in range(TT):
                    for k in range(DK):
                        mm = nc.tensor.matmul(kv_ps[:, t, :], xT[:, k, t * P:(t + 1) * P], wqkv[:, k, KH:3 * KH],
                                              start=(k == 0), stop=(k == DK - 1))
                mm.then_inc(qkv_done, 1)

            def transposes(n):
                pe.wait_ge(x2_made, n + 1)
                for k in range(DK):
                    for t in range(TT):
                        mm = nc.tensor.transpose(x2T_ps[k][:, t * P:(t + 1) * P], x2[:, t, k * P:(k + 1) * P], ident[:, :])
                mm.then_inc(tr_done, 1)

            def scores(n, first=False):
                pe.wait_ge(elu_made, n + 1)
                if not first:
                    pe.wait_ge(den_step, 2 * n - 1)
                for t in range(TT):
                    nc.tensor.matmul(s_ps[:, t, :], kT[:, t * P:(t + 1) * P], qT[:, t * P:(t + 1) * P], start=True, stop=True)
                for t in range(TT):
                    mm = nc.tensor.matmul(delta_ps[:, t, :], kv1[:, t, 0:KH], kv1[:, t, KH:2 * KH + 1], start=True, stop=True)
                mm.then_inc(sd_done, 1)

            def chunk(n, first=False, last=False):
                if not first:
                    scores(n)
                pe.wait_ge(got_ctx, 16 * (n + 1))
                if last:
                    pe.wait_ge(tail_filled, 1)
                if not first:
                    pe.wait_ge(u_copied, n)
                    pe.wait_ge(x2T_copied, n)
                for t in range(LAST_CTX if last else TT):
                    for k in range(DK):
                        mm = nc.tensor.matmul(u_ps[:, t, :], ctx_chunk[:, k, t * P:(t + 1) * P], wvo[:, k, :],
                                              start=(k == 0), stop=(k == DK - 1))
                mm.then_inc(u_done, 1)
                pe.wait_ge(sT_made, n + 1)
                pe.wait_ge(state_step, (TT + 1) * (n + 1))
                for t in range(TT):
                    cols = slice(t * P, (t + 1) * P)
                    nc.tensor.matmul(numT_ps[:, cols], kv1[:, t, KH:2 * KH + 1], sT[:, t, :], start=True, stop=False)
                    mm = nc.tensor.matmul(numT_ps[:, cols], state[:, t, :], qT[:, cols], start=False, stop=True)
                mm.then_inc(num_done, 1)
                if not last:
                    qkv(n + 1)
                pe.wait_ge(num_copied, n + 1)
                if not first:
                    pe.wait_ge(res1_made, n)
                for t in range(TT):
                    cols = slice(t * P, (t + 1) * P)
                    nc.tensor.matmul(y_ps[:, t, :], numT[0:KH, cols], wo[:, :], start=True, stop=True)
                for t in range(TT):
                    cols = slice(t * P, (t + 1) * P)
                    mm = nc.tensor.matmul(den_ps[:, t:t + 1], numT[:, cols], den_pick[:, :], start=True, stop=True)
                mm.then_inc(y_done, 1)
                if not first:
                    pe.wait_ge(u_copied, n + 1)
                    transposes(n - 1)

            pe.sem_inc(tr_done, 1)
            pe.wait_ge(got_wqkv, 16)
            qkv(0)
            pe.wait_ge(got_wv, 16)
            pe.wait_ge(got_wout, 16)
            for c in range(DK):
                for k in range(IK):
                    mm = nc.tensor.matmul(wvo_ps[c], wv[:, k, c * P:(c + 1) * P], wout[:, k, :],
                                          start=(k == 0), stop=(k == IK - 1))
            mm.then_inc(wvo_done, 1)
            pe.wait_ge(dve_consts, 1)
            scores(0, first=True)
            pe.wait_ge(wvo_copied, 1)
            pe.wait_ge(ident_made, 1)
            pe.wait_ge(got_wo, 16)
            chunk(0, first=True)
            with pe.Fori(1, CHUNKS - 1) as n:
                chunk(n)
            chunk(CHUNKS - 1, last=True)
            def ffn(n, finer=False, first=False):
                def bank(slot, b):
                    return ps[:, 2 * (slot % PAIRS) + b, :]

                def pair_free(slot):
                    if slot == 0:
                        pass
                    elif slot < PAIRS and first:
                        pe.wait_ge(res1_made, CHUNKS)
                    elif slot < PAIRS:
                        pe.wait_ge(out_read, OUT_SLOTS * (n - 1) + slot)
                    elif slot < PAIRS + GATE_SLOTS:
                        pe.wait_ge(gate_made, GATE_SLOTS * n + slot - PAIRS + 1)
                    else:
                        pe.wait_ge(gelu_made, 2 * FK * n + 2 * (slot - PAIRS - GATE_SLOTS + 1))

                def weights_in(pieces):
                    if first:
                        pe.wait_ge(w_rounded, pieces)

                piece = LO_PIECES * (n - CHUNKS)
                pe.wait_ge(xs_ready, n + 1)
                weights_in(-(-H1 // ECOLS))
                for m in range(GATE_SLOTS):
                    pair_free(m)
                    if finer:
                        pe.wait_ge(lo_made, piece + 1)
                        piece += 1
                        for b in range(2):
                            for k in range(DK):
                                c = (DK * b + k) * P
                                for part in range(2):
                                    mm = nc.tensor.matmul(bank(m, b), w_lo[:, c:c + P], xs[part][:, k, :],
                                                          start=(k == 0 and part == 0), stop=False)
                        mm.then_inc(lo_used, 1)
                    for b, w in enumerate((W1, W2)):
                        for k in range(DK):
                            c = w + k * F + m * P
                            for part in range(2):
                                mm = nc.tensor.matmul(bank(m, b), W[:, c:c + P], xs[part][:, k, :],
                                                      start=(k == 0 and part == 0 and not finer),
                                                      stop=(k == DK - 1 and part == 1))
                    mm.then_inc(slot_done, 1)

                for layer, (w, h) in enumerate(((H1, h1), (H2, h2))):
                    if layer == 0:
                        weights_in(EARLY)
                    for j in range(HID_SLOTS):
                        slot = GATE_SLOTS + layer * HID_SLOTS + j
                        pair_free(slot)
                        if finer:
                            pe.wait_ge(h_ready, TILES * n + (layer + 1) * FK)
                            for b in range(2):
                                for k0 in (0, FK // 2):
                                    pe.wait_ge(lo_made, piece + 1)
                                    piece += 1
                                    for k in range(FK // 2):
                                        for part in range(2):
                                            mm = nc.tensor.matmul(bank(slot, b), w_lo[:, k * P:(k + 1) * P],
                                                                  h[part][:, k0 + k, :],
                                                                  start=(k0 + k == 0 and part == 0), stop=False)
                                    mm.then_inc(lo_used, 1)
                        for k in range(FK):
                            if j == 0:
                                pe.wait_ge(h_ready, TILES * n + layer * FK + k + 1)
                            if layer == 1 and j == 0:
                                weights_in(EARLY + k + 1)
                            for b in range(2):
                                c = w + k * F + (2 * j + b) * P
                                for part in range(2):
                                    mm = nc.tensor.matmul(bank(slot, b), W[:, c:c + P], h[part][:, k, :],
                                                          start=(k == 0 and part == 0 and not finer),
                                                          stop=(k == FK - 1 and part == 1))
                        mm.then_inc(slot_done, 1)
                        if first and layer == 0 and j == 1:
                            pe.wait_ge(x2T_copied, CHUNKS)
                            transposes(CHUNKS - 1)

                weights_in(PIECES)
                for pair in range(OUT_SLOTS):
                    slot = SLOTS - OUT_SLOTS + pair
                    pair_free(slot)
                    if finer:
                        pe.wait_ge(h_ready, TILES * (n + 1))
                        for k0 in range(0, FK, 2):
                            pe.wait_ge(lo_made, piece + 1)
                            piece += 1
                            for b in range(2):
                                t = 2 * pair + b
                                for k in range(2):
                                    for part in range(2):
                                        mm = nc.tensor.matmul(bank(slot, b)[:, 0:D], h1[part][:, k0 + k, t * P:(t + 1) * P],
                                                              w_lo[:, k * D:(k + 1) * D],
                                                              start=(k0 + k == 0 and part == 0), stop=False)
                            mm.then_inc(lo_used, 1)
                    for k in range(FK):
                        if pair == 0:
                            pe.wait_ge(h_ready, TILES * n + 2 * FK + k + 1)
                        for b in range(2):
                            t = 2 * pair + b
                            for part in range(2):
                                mm = nc.tensor.matmul(bank(slot, b)[:, 0:D], h1[part][:, k, t * P:(t + 1) * P],
                                                      W[:, W3 + k * D:W3 + (k + 1) * D],
                                                      start=(k == 0 and part == 0 and not finer),
                                                      stop=(k == FK - 1 and part == 1))
                    mm.then_inc(slot_done, 1)

            ffn(0, first=True)
            with pe.Fori(1, CHUNKS - 1) as n:
                ffn(n)
            pe.wait_ge(weights_looked, 1)
            nc.tensor.matmul(flag_ps, unequal_sum[:, :], ones[:, :], start=True, stop=True).then_inc(flag_sum, 1)
            ffn(CHUNKS - 1)
            pe.wait_ge(flag_made, 1)
            finer = pe.value_load(flag[0:1, 0:1], min_val=0, max_val=1)
            with pe.If(finer > 0):
                with pe.Fori(CHUNKS, 2 * CHUNKS) as n:
                    ffn(n, finer=True)


_IN = ["x_tok", "x_feat", "ctx_feat", "wqkv", "wo", "wv", "wout", "bout", "ffn_w", "scales", "w3s"]


def kernel(x, ctx_1024, L0_attn_Wq, L0_attn_Wk, L0_attn_Wv, L0_attn_Wo, L0_xattn_Wq, L0_xattn_Wkv, L0_xattn_Wout,
           L0_xattn_bout, L0_ffn_w1_w, L0_ffn_w1_s, L0_ffn_w2_w, L0_ffn_w2_s, L0_ffn_h1_w, L0_ffn_h1_s, L0_ffn_h2_w,
           L0_ffn_h2_s, L0_ffn_w3_w, L0_ffn_w3_s):
    import numpy as np
    import concourse.bacc as bacc
    from concourse.bass_utils import run_bass_kernel_spmd

    def features_on_partitions(a):
        a = np.asarray(a)
        return a.reshape(-1, P, a.shape[1]).transpose(1, 0, 2)

    x0 = np.asarray(x)[0]
    wkv = np.asarray(L0_xattn_Wkv)
    ffn = [L0_ffn_w1_w, L0_ffn_w2_w, L0_ffn_h1_w, L0_ffn_h2_w, L0_ffn_w3_w]
    arrays = {
        "x_tok": x0.reshape(CHUNKS, TT, P, D).transpose(0, 2, 1, 3),
        "x_feat": x0.T.reshape(DK, P, CHUNKS, T).transpose(2, 1, 0, 3),
        "ctx_feat": features_on_partitions(np.asarray(ctx_1024)[0].T),
        "wqkv": features_on_partitions(np.concatenate([np.asarray(w).T for w in (L0_attn_Wq, L0_attn_Wk, L0_attn_Wv)], axis=1)),
        "wo": np.asarray(L0_attn_Wo).T,
        "wv": features_on_partitions(wkv[:, INNER:].T),
        "wout": features_on_partitions(L0_xattn_Wout),
        "bout": np.asarray(L0_xattn_bout),
        "ffn_w": np.concatenate([features_on_partitions(np.asarray(w).T).reshape(P, -1) for w in ffn], axis=1),
        "scales": np.concatenate([np.asarray(s).reshape(FK, P).T for s in (L0_ffn_w1_s, L0_ffn_w2_s, L0_ffn_h1_s, L0_ffn_h2_s)], axis=1),
        "w3s": np.asarray(L0_ffn_w3_s),
    }
    arrays = {name: np.ascontiguousarray(a) for name, a in arrays.items()}
    nc = bacc.Bacc("TRN2", target_bir_lowering=False, num_devices=1)
    args = [nc.dram_tensor("in_" + name, arrays[name].shape, mybir.dt.from_np(arrays[name].dtype), kind="ExternalInput").ap() for name in _IN]
    out = nc.dram_tensor("layer_out", (CHUNKS, P, TT * D), F32, kind="ExternalOutput").ap()
    decoder_layer(nc, *args, out)
    r = run_bass_kernel_spmd(nc, [{"in_" + name: a for name, a in arrays.items()}], core_ids=[0])
    got = r.results[0]["layer_out"]
    return got.reshape(CHUNKS, P, TT, D).transpose(0, 2, 1, 3).reshape(1, S, D)
```

```python
from contextlib import ExitStack

import concourse.bass as bass
from concourse import mybir

ALU = mybir.AluOpType
ACT = mybir.ActivationFunctionType
AX = mybir.AxisListType
F32 = mybir.dt.float32
F32R = mybir.dt.float32r
I32 = mybir.dt.int32

P = 128
S = 2048
SC = 1601
D = 256
DK = D // P
KH = 64
INNER = 1024
IK = INNER // P
F = 1024
FK = F // P
T = 512
CHUNKS = S // T
MEAN_TILE = -(-SC // P)
TT = T // P
LAST_CTX = MEAN_TILE + 1 - (CHUNKS - 1) * TT
LAST_KEYS = SC - (CHUNKS - 1) * T
assert 0 < LAST_CTX <= TT
EPS = 1e-5
DEN_EPS = 1e-6

W1, W2, H1, H2, W3 = 0, DK * F, 2 * DK * F, 2 * DK * F + FK * F, 2 * DK * F + 2 * FK * F
WCOLS = W3 + FK * D
EARLY = 2 * CHUNKS
ECOLS = H2 // EARLY
LATE = 10
LCOLS = (WCOLS - H2) // LATE
assert ECOLS * EARLY == H2 and LCOLS * LATE == WCOLS - H2
PIECES = EARLY + LATE

PAIRS = 3
GATE_SLOTS = FK
HID_SLOTS = FK // 2
OUT_SLOTS = TT // 2
SLOTS = GATE_SLOTS + 2 * HID_SLOTS + OUT_SLOTS
TILES = 3 * FK
HF = 3
LAST_PARTS = [(0, 2), (2, 3), (3, 4)]
STORES = CHUNKS - 1 + len(LAST_PARTS)
WARM_UP = 2
LO_PIECES = GATE_SLOTS + 2 * HID_SLOTS * 4 + OUT_SLOTS * 4
assert SLOTS % PAIRS == 0 and TILES % HF == 0 and LCOLS == F


def decoder_layer(nc, x_tok, x_feat, ctx_feat, wqkv_d, wo_d, wv_d, wout_d, bout_d, ffn_w, scales_d, w3s_d, out):
    with ExitStack() as ctx:
        def sem(name):
            return ctx.enter_context(nc.semaphore(name))

        def keep(name, shape, dt=F32):
            return ctx.enter_context(nc.sbuf_tensor(name, shape, dt))

        W = keep("W", [P, WCOLS], F32R)
        x2_all = keep("x2_all", [P, CHUNKS, TT * D])
        x2T_all = keep("x2T_all", [P, DK, S])
        scales = keep("scales", [P, 4 * FK])
        w3s = keep("w3s", [P, D])
        stats = keep("stats", [P, TT, 6])
        mv = [keep(f"mv{i}", [P, TT, 2]) for i in range(3)]
        rstd = [keep(f"rstd{i}", [P, TT]) for i in range(3)]
        shift = [keep(f"shift{i}", [P, TT]) for i in range(2)]
        eps = keep("eps", [P, TT])
        zero = keep("zero", [P, TT])
        minus_half = keep("minus_half", [P, TT])
        unequal = keep("unequal", [P, PIECES])
        unequal_sum = keep("unequal_sum", [P, 1])
        ones = keep("ones", [P, 1])
        flag = keep("flag", [1, 1], I32)

        def area(stack):
            return lambda name, shape, dt=F32: stack.enter_context(nc.sbuf_tensor(name, shape, dt))

        with ExitStack() as attention:
            with ExitStack() as low:
                sb = area(low)
                e_qk = sb("e_qk", [P, T])
                r_qk = sb("r_qk", [P, T])
                xT = sb("xT", [P, DK, T])
                ctx_chunk = sb("ctx_chunk", [P, DK, T])
                e_k = sb("e_k", [P, TT, KH])
                r_k = sb("r_k", [P, TT, KH])
                xt = sb("xt", [P, TT, D])
                wqkv = sb("wqkv", [P, DK, 3 * KH])
                wo = sb("wo", [KH, D])
                wvo = sb("wvo", [P, DK, D])
                mask = sb("mask", [P, TT, P])
                qT = sb("qT", [KH, T])
                kT = sb("kT", [KH, T])
                kv1 = sb("kv1", [P, TT, 2 * KH + 1])
                sT = sb("sT", [P, TT, P])
                state = sb("state", [KH, TT + 1, KH + 1])
                numT = sb("numT", [KH + 1, T])
                den = sb("den", [P, TT])
                rden = sb("rden", [P, TT])
                den_pick = sb("den_pick", [KH + 1, 1])
                ctx_sums = sb("ctx_sums", [P, DK, CHUNKS])
                ctx_sum = sb("ctx_sum", [P, DK])
                ctx_again = sb("ctx_again", [P, DK, T])
                ctx_mean = sb("ctx_mean", [P, DK])
            sb = area(attention)
            sb("below_h2", [P, 2 * DK * T + HF * T + 2 * T + TT * D + 2 * FK * T])
            with ExitStack() as early:
                wv = area(early)("wv", [P, IK, D])
                wout = area(early)("wout", [P, IK, D])
            res1 = sb("res1", [P, TT, D])
            ub = sb("ub", [P, TT, D])
            res2 = sb("res2", [P, TT, D])
            x2 = sb("x2", [P, TT, D])
            stage = [sb(f"stage{i}", [P, ECOLS]) for i in range(2)]
            bout = sb("bout", [P, D])
            ident = sb("ident", [P, P])

        with ExitStack() as feed_forward:
            sb = area(feed_forward)
            xs = [sb(f"xs_{p}", [P, DK, T], F32R) for p in ("hi", "lo")]
            hf = [sb(f"hf{i}", [P, T]) for i in range(HF)]
            with ExitStack() as first_chunk:
                late_stage = [area(first_chunk)(f"late_stage{i}", [P, LCOLS]) for i in range(2)]
            w_again = sb("w_again", [P, T])
            w_lo = sb("w_lo", [P, T], F32R)
            fin = sb("fin", [P, TT, D])
            h1 = [sb(f"h1_{p}", [P, FK, T], F32R) for p in ("hi", "lo")]
            h2 = [sb(f"h2_{p}", [P, FK, T], F32R) for p in ("hi", "lo")]

        ps = ctx.enter_context(nc.psum_tensor("ps", [P, 8, 512], F32))
        QK, KV, SC_B, ND_B, Y_B, U_B = 0, 1, 2, 3, 4, 6
        kv_ps = ps[:, KV, :].rearrange("p (t c) -> p t c", t=TT)
        s_ps = ps[:, SC_B, :].rearrange("p (t c) -> p t c", t=TT)
        y_ps = ps[:, Y_B:Y_B + 2, :].rearrange("p b (t c) -> p (b t) c", t=2)
        u_ps = ps[:, U_B:U_B + 2, :].rearrange("p b (t c) -> p (b t) c", t=2)
        delta_ps = ps[0:KH, ND_B, 0:TT * (KH + 1)].rearrange("p (t c) -> p t c", t=TT)
        numT_ps = ps[0:KH + 1, ND_B, :]
        den_ps = [ps[:, bank, 0:TT] for bank in (QK, ND_B)]
        wvo_ps = [ps[:, U_B + c, 0:D] for c in range(DK)]
        x2T_ps = [ps[:, U_B + c, :] for c in range(DK)]
        flag_ps = ps[0:1, U_B, 0:1]

        got_xT_rest = sem("got_xT_rest")
        got_xT, got_xt, got_wqkv, got_wo = sem("got_xT"), sem("got_xt"), sem("got_wqkv"), sem("got_wo")
        got_ctx, got_bout = sem("got_ctx"), sem("got_bout")
        got_wv, got_wout = [[sem(f"got_{w}_{half}") for half in range(2)] for w in ("wv", "wout")]
        got_scales, got_w3s = sem("got_scales"), sem("got_w3s")
        got_stage = [sem("got_stage0"), sem("got_stage1")]
        got_late = [sem("got_late0"), sem("got_late1")]
        got_again, stored = sem("got_again"), sem("stored")
        x2_kept = sem("x2_kept")
        ident_zero, ident_made = sem("ident_zero"), sem("ident_made")
        mask_one, mask_made = sem("mask_one"), sem("mask_made")
        zeros_made, dve_consts = sem("zeros_made"), sem("dve_consts")
        wvo_done, qkv_done, sd_done, u_done = sem("wvo_done"), sem("qkv_done"), sem("sd_done"), sem("u_done")
        num_done, den_done, y_done, tr_done = sem("num_done"), sem("den_done"), sem("y_done"), sem("tr_done")
        flag_sum = sem("flag_sum")
        wvo_copied, qkv_acted, u_copied = sem("wvo_copied"), sem("qkv_acted"), sem("u_copied")
        num_copied, x2T_copied, w_rounded = sem("num_copied"), sem("x2T_copied"), sem("w_rounded")
        x1_made, x2_made, ctx_summed = sem("x1_made"), sem("x2_made"), sem("ctx_summed")
        mean_step, tail_filled = sem("mean_step"), sem("tail_filled")
        sT_made, state_step, elu_made = sem("sT_made"), sem("state_step"), sem("elu_made")
        den_step, res1_made, res2_made = sem("den_step"), sem("res1_made"), sem("res2_made")
        stats_made = [sem(f"stats{i}_made") for i in (1, 2, 3)]
        mv_made = [sem(f"mv{i}_made") for i in (1, 2, 3)]
        w_looked, weights_looked, flag_made = sem("w_looked"), sem("weights_looked"), sem("flag_made")
        ub_made = sem("ub_made")
        pool_consts, pool_step = sem("pool_consts"), sem("pool_step")
        norm_ready = [sem(f"norm{i}_ready") for i in (1, 2, 3)]
        slot_done = sem("slot_done")
        xs_hi_made, xs_ready = sem("xs_hi_made"), sem("xs_ready")
        silu_made, gate_made = sem("silu_made"), sem("gate_made")
        gelu_made = sem("gelu_made")
        hi_made, h_ready = sem("hi_made"), sem("h_ready")
        out_read = sem("out_read")
        tile_done, tile_read = sem("tile_done"), sem("tile_read")
        out_added, out_made = sem("out_added"), sem("out_made")
        lo_made, lo_used = sem("lo_made"), sem("lo_used")

        block = ctx.enter_context(nc.Block())


        @block.sync
        def _(sp):
            sp.dma_start(xT[:, 0, :], x_feat[0][:, 0, :]).then_inc(got_xT, 16)
            sp.dma_start(xT[:, 1:DK, :], x_feat[0][:, 1:DK, :]).then_inc(got_xT_rest, 16)
            for half in range(2):
                k = slice(half * IK // 2, (half + 1) * IK // 2)
                sp.dma_start(wv[:, k, :], wv_d[:, k, :]).then_inc(got_wv[half], 16)
                sp.dma_start(wout[:, k, :], wout_d[:, k, :]).then_inc(got_wout[half], 16)

            def load_piece(n, i):
                sp.dma_start(stage[i][:, :], ffn_w[:, bass.ds((2 * n + i) * ECOLS, ECOLS)]).then_inc(got_stage[i], 16)

            def load_xT(n):
                sp.wait_ge(qkv_done, n)
                sp.dma_start(xT[:, :, :], x_feat[bass.ds(n, 1)].rearrange("a p k t -> (a p) k t")).then_inc(got_xT, 16)

            def load_ctx(n, cols=T):
                sp.wait_ge(u_done, n)
                sp.wait_ge(ctx_summed, n)
                sp.dma_start(ctx_chunk[:, :, 0:cols], ctx_feat[:, :, bass.ds(n * T, cols)]).then_inc(got_ctx, 16)

            def keep_x2(n):
                sp.wait_ge(x2_made, n + 1)
                sp.dma_start(x2_all[:, bass.ds(n, 1), :].rearrange("p a c -> p (a c)"),
                             x2[:, :, :].rearrange("p t d -> p (t d)")).then_inc(x2_kept, 16)

            def chunk(n, ctx_cols=T, xT_left=True, first=False, last=False):
                if xT_left:
                    load_xT(n + 2)
                if not first:
                    sp.wait_ge(w_looked, 2 * n)
                    load_piece(n, 1)
                if not last:
                    load_ctx(n + 1, ctx_cols)
                    sp.wait_ge(res1_made, n + 1)
                    sp.dma_start(xt[:, :, :], x_tok[bass.ds(n + 1, 1)].rearrange("a p t d -> (a p) t d")).then_inc(got_xt, 16)
                    sp.wait_ge(w_looked, 2 * n + 1)
                    load_piece(n + 1, 0)
                if not first and not last:
                    keep_x2(n - 1)

            load_piece(0, 0)
            load_xT(1)
            load_piece(0, 1)
            chunk(0, first=True)
            with sp.Fori(1, CHUNKS - 2) as n:
                chunk(n)
            chunk(CHUNKS - 2, ctx_cols=LAST_KEYS, xT_left=False)
            chunk(CHUNKS - 1, xT_left=False, last=True)

            sp.wait_ge(res1_made, CHUNKS)
            sp.wait_ge(u_done, CHUNKS)
            for i in range(LATE):
                if i in (2, 4):
                    keep_x2(CHUNKS - 3 + i // 2)
                if i >= 2:
                    sp.wait_ge(w_looked, EARLY + i - 1)
                c = H2 + i * LCOLS
                sp.dma_start(late_stage[i % 2][:, :], ffn_w[:, c:c + LCOLS]).then_inc(got_late[i % 2], 16)

            def store(n, made, c0, c1):
                sp.wait_ge(out_made, made)
                sp.dma_start(out[bass.ds(n, 1), :, c0:c1].rearrange("a p c -> (a p) c"),
                             fin[:, c0 // D:c1 // D, :].rearrange("p t d -> p (t d)")).then_inc(stored, 16)

            def stores_of_last(made):
                for part, (t0, t1) in enumerate(LAST_PARTS):
                    store(CHUNKS - 1, made + part, t0 * D, t1 * D)

            with sp.Fori(0, CHUNKS - 1) as n:
                store(n, n + 1, 0, TT * D)
            stores_of_last(CHUNKS)

            gates = ffn_w[:, W1:H1].rearrange("p (k o) -> p k o", o=F)
            hidden = [ffn_w[:, h:h + FK * F].rearrange("p (k o) -> p k o", o=F) for h in (H1, H2)]

            def lo_pieces():
                for m in range(GATE_SLOTS):
                    yield gates[:, :, m * P:(m + 1) * P]
                for w in hidden:
                    for m in range(FK):
                        for k in (0, FK // 2):
                            yield w[:, k:k + FK // 2, m * P:(m + 1) * P]
                for _ in range(OUT_SLOTS):
                    for k in range(0, FK, 2):
                        yield ffn_w[:, W3 + k * D:W3 + (k + 2) * D]

            def load_again(n):
                for i, piece in enumerate(lo_pieces()):
                    if i or n is not CHUNKS:
                        sp.wait_ge(lo_made, LO_PIECES * (n - CHUNKS) + i)
                    dst = w_again[:, :]
                    if len(piece.shape) == 3:
                        dst = dst.rearrange("p (k o) -> p k o", o=P)
                    sp.dma_start(dst, piece).then_inc(got_again, 16)
                    if i == GATE_SLOTS + HID_SLOTS * 4 and n is not CHUNKS:
                        store(n - 1 - CHUNKS, n + STORES - CHUNKS, 0, TT * D)

            sp.wait_ge(flag_made, 1)
            finer = sp.value_load(flag[0:1, 0:1], min_val=0, max_val=1)
            with sp.If(finer > 0):
                sp.wait_ge(stored, 16 * STORES)
                load_again(CHUNKS)
                with sp.Fori(CHUNKS + 1, 2 * CHUNKS) as n:
                    load_again(n)
                stores_of_last(CHUNKS + STORES)
                sp.wait_ge(stored, 2 * 16 * STORES)
            with sp.Else():
                sp.wait_ge(stored, 16 * STORES)

        @block.gpsimd
        def _(pool):
            nc.gpsimd.memset(ident[:, :], 0.0).then_inc(ident_zero, 1)
            nc.gpsimd.memset(mask[:, :, :], 1.0).then_inc(mask_one, 1)
            nc.gpsimd.memset(eps[:, :], EPS)
            nc.gpsimd.memset(zero[:, :], 0.0)
            nc.gpsimd.memset(minus_half[:, :], -0.5).then_inc(pool_consts, 1)
            pool.wait_ge(ident_zero, 1)
            nc.gpsimd.affine_select(out=ident[:, :], in_=ident[:, :], compare_op=ALU.not_equal, fill=1.0,
                                    base=0, pattern=[[-1, P]], channel_multiplier=1).then_inc(ident_made, 1)
            pool.wait_ge(mask_one, 1)
            nc.gpsimd.affine_select(out=mask[:, :, :], in_=mask[:, :, :], compare_op=ALU.is_ge, fill=0.0,
                                    base=0, pattern=[[0, TT], [1, P]], channel_multiplier=-1).then_inc(mask_made, 1)
            pool.wait_ge(pool_consts, 1)

            def factors(which, n, done, c0=0, c1=TT):
                cols = slice(c0, c1)
                pool.wait_ge(mv_made[which], n + 1)
                nc.gpsimd.tensor_tensor(rstd[which][:, cols], mv[which][:, cols, 1], eps[:, cols], ALU.add).then_inc(pool_step, 1)
                last = which == 2
                if not last:
                    nc.gpsimd.tensor_tensor(shift[which][:, cols], zero[:, cols], mv[which][:, cols, 0], ALU.subtract)
                pool.wait_ge(pool_step, done + 1)
                nc.gpsimd.tensor_tensor(rstd[which][:, cols], rstd[which][:, cols], minus_half[:, cols],
                                        ALU.pow).then_inc(norm_ready[which] if last else pool_step, 1)
                if not last:
                    pool.wait_ge(pool_step, done + 2)
                    nc.gpsimd.tensor_tensor(shift[which][:, cols], shift[which][:, cols], rstd[which][:, cols],
                                            ALU.mult).then_inc(norm_ready[which], 1)

            def add_bias(n):
                pool.wait_ge(u_copied, n + 1)
                nc.gpsimd.tensor_tensor(ub[:, :, :], ub[:, :, :], bout[:, :].unsqueeze(1).to_broadcast([P, TT, D]),
                                        ALU.add).then_inc(ub_made, 1)

            def both_factors(n):
                factors(0, n, 4 * n)
                factors(1, n, 4 * n + 2)

            pool.wait_ge(got_bout, 16)
            add_bias(0)
            with pool.Fori(1, CHUNKS) as n:
                both_factors(n - 1)
                add_bias(n)
            both_factors(CHUNKS - 1)

            def third_norms(done):
                with pool.Fori(0, CHUNKS - 1) as n:
                    factors(2, done + n, 4 * CHUNKS + done + n)
                for part, (t0, t1) in enumerate(LAST_PARTS):
                    n = done + CHUNKS - 1 + part
                    factors(2, n, 4 * CHUNKS + n, t0, t1)

            third_norms(0)
            pool.wait_ge(flag_made, 1)
            finer = pool.value_load(flag[0:1, 0:1], min_val=0, max_val=1)
            with pool.If(finer > 0):
                third_norms(STORES)

        @block.scalar
        def _(act):
            act.sem_inc(x2T_copied, 2)
            act.dma_start(wqkv[:, :, :], wqkv_d).then_inc(got_wqkv, 16)
            act.dma_start(wo[:, :], wo_d).then_inc(got_wo, 16)
            act.dma_start(bout[:, :], bout_d.partition_broadcast(P)).then_inc(got_bout, 16)
            act.dma_start(w3s[:, :], w3s_d.partition_broadcast(P)).then_inc(got_w3s, 16)
            act.dma_start(scales[:, :], scales_d).then_inc(got_scales, 16)
            act.dma_start(ctx_chunk[:, :, :], ctx_feat[:, :, 0:T]).then_inc(got_ctx, 16)
            act.dma_start(xt[:, :, :], x_tok[0]).then_inc(got_xt, 16)

            def qkv_parts(m, first=False):
                act.wait_ge(qkv_done, m + 1)
                nc.scalar.activation(e_qk[:, :], ps[:, QK, :], ACT.Exp)
                nc.scalar.activation(r_qk[:, :], ps[:, QK, :], ACT.Relu)
                nc.scalar.activation(e_k[:, :, :], kv_ps[:, :, 0:KH], ACT.Exp)
                nc.scalar.activation(r_k[:, :, :], kv_ps[:, :, 0:KH], ACT.Relu)
                if not first:
                    act.wait_ge(num_done, m)
                nc.scalar.copy(kv1[:, :, KH:2 * KH], kv_ps[:, :, KH:2 * KH]).then_inc(qkv_acted, 1)

            def round_piece(n, i):
                act.wait_ge(got_stage[i], 16 * (n + 1))
                nc.scalar.copy(W[:, bass.ds((2 * n + i) * ECOLS, ECOLS)], stage[i][:, :]).then_inc(w_rounded, 1)

            def round_late(i):
                act.wait_ge(got_late[i % 2], 16 * (i // 2 + 1))
                c = H2 + i * LCOLS
                nc.scalar.copy(W[:, c:c + LCOLS], late_stage[i % 2][:, :]).then_inc(w_rounded, 1)

            def first_norm(n):
                act.wait_ge(norm_ready[0], n + 1)
                for t in range(TT):
                    a = nc.scalar.activation(res1[:, t, :], res1[:, t, :], ACT.Identity, scale=rstd[0][:, t:t + 1],
                                             bias=shift[0][:, t:t + 1])
                a.then_inc(x1_made, 1)

            def second_norm(n, first=False):
                act.wait_ge(tr_done, n + 1)
                if not first:
                    act.wait_ge(x2_kept, 16 * n)
                act.wait_ge(norm_ready[1], n + 1)
                for t in range(TT):
                    a = nc.scalar.activation(x2[:, t, :], res2[:, t, :], ACT.Identity, scale=rstd[1][:, t:t + 1],
                                             bias=shift[1][:, t:t + 1])
                a.then_inc(x2_made, 1)

            def sum_ctx(n, keys=T, first=False):
                act.wait_ge(got_ctx, 16 * (n + 1))
                if not first:
                    act.wait_ge(ctx_summed, n)
                for k in range(DK):
                    a = nc.scalar.activation(ctx_again[:, k, 0:keys], ctx_chunk[:, k, 0:keys], ACT.Copy,
                                             accum_out=ctx_sums[:, k, bass.ds(n, 1)])
                a.then_inc(ctx_summed, 1)

            def keep_x2T(n):
                act.wait_ge(tr_done, n + 2)
                for k in range(DK):
                    c = nc.scalar.copy(x2T_all[:, k, bass.ds(n * T, T)], x2T_ps[k])
                c.then_inc(x2T_copied, 1)

            def chunk(n, step):
                last = step == CHUNKS - 1
                sum_ctx(n, LAST_KEYS if last else T, first=step == 0)
                if step >= 2 and not last:
                    second_norm(n - 2, first=step == 2)
                act.wait_ge(elu_made, n + 1)
                if not last:
                    qkv_parts(n + 1)
                act.wait_ge(num_done, n + 1)
                nc.scalar.copy(numT[:, :], numT_ps).then_inc(num_copied, 1)
                if last:
                    act.wait_ge(x2T_copied, 3)
                    split_x_hi(0)
                    second_norm(n - 2)
                if step >= 1:
                    first_norm(n - 1)
                if not last:
                    round_piece(n, 0)
                act.wait_ge(u_done, n + 1)
                if step >= 1:
                    act.wait_ge(res2_made, n)
                if not last:
                    nc.scalar.copy(ub[:, :, :], u_ps).then_inc(u_copied, 1)
                    round_piece(n, 1)
                else:
                    nc.scalar.copy(ub[:, 0:LAST_CTX, :], u_ps[:, 0:LAST_CTX, :])
                    mean_u = u_ps[:, LAST_CTX - 1, :].unsqueeze(1).to_broadcast([P, TT - LAST_CTX, D])
                    nc.scalar.copy(ub[:, LAST_CTX:TT, :], mean_u).then_inc(u_copied, 1)
                if step >= 2 and not last:
                    keep_x2T(n - 2)

            def split_x_hi(n):
                nc.scalar.copy(xs[0][:, :, :], x2T_all[:, :, bass.ds(n * T, T)]).then_inc(xs_hi_made, 1)

            qkv_parts(0, first=True)
            act.wait_ge(wvo_done, 1)
            for c in range(DK):
                cp = nc.scalar.copy(wvo[:, c, :], wvo_ps[c])
            cp.then_inc(wvo_copied, 1)
            chunk(0, 0)
            chunk(1, 1)
            with act.Fori(2, CHUNKS - 1) as n:
                chunk(n, 2)
            chunk(CHUNKS - 1, CHUNKS - 1)

            def hi(n, tile):
                h = h1 if tile // FK != 1 else h2
                nc.scalar.copy(h[0][:, tile % FK, :], hf[tile % HF][:, :]).then_inc(hi_made, 1)

            def ffn(n, base=0, first=False, last=False):
                for m in range(GATE_SLOTS + 1):
                    if m < GATE_SLOTS:
                        act.wait_ge(slot_done, SLOTS * n + m + 1)
                        if m >= HF:
                            act.wait_ge(h_ready, TILES * n + m - HF + 1)
                        nc.scalar.activation(hf[m % HF][:, :], ps[:, 2 * (m % PAIRS), :], ACT.Silu,
                                             scale=scales[:, m:m + 1]).then_inc(silu_made, 1)
                    if m:
                        act.wait_ge(gate_made, GATE_SLOTS * n + m)
                        hi(n, m - 1)
                    if first and m == 5:
                        round_piece(CHUNKS - 1, 0)
                    if first and m == GATE_SLOTS:
                        keep_x2T(CHUNKS - 3)
                        round_piece(CHUNKS - 1, 1)
                        second_norm(CHUNKS - 2)
                        first_norm(CHUNKS - 1)
                for layer in range(2):
                    if layer == 1 and not last:
                        act.wait_ge(slot_done, SLOTS * n + GATE_SLOTS)
                        split_x_hi(n + 1 - base)
                    for j in range(HID_SLOTS):
                        slot = GATE_SLOTS + layer * HID_SLOTS + j
                        act.wait_ge(slot_done, SLOTS * n + slot + 1)
                        for b in range(2):
                            tile = FK * (layer + 1) + 2 * j + b
                            act.wait_ge(h_ready, TILES * n + tile - HF + 1)
                            s = FK * (layer + 2) + 2 * j + b
                            nc.scalar.activation(hf[tile % HF][:, :], ps[:, 2 * (slot % PAIRS) + b, :], ACT.Gelu,
                                                 scale=scales[:, s:s + 1]).then_inc(gelu_made, 1)
                        if first and layer == 0 and j == 0:
                            act.wait_ge(res2_made, CHUNKS)
                        if first and layer == 0 and j == HID_SLOTS - 1:
                            act.wait_ge(x2_kept, 16 * CHUNKS)
                        for b in range(2):
                            tile = FK * (layer + 1) + 2 * j + b
                            act.wait_ge(gelu_made, 2 * FK * n + tile - FK + 1)
                            hi(n, tile)
                        if first and layer == 0 and j == 1:
                            second_norm(CHUNKS - 1)
                        if first and layer == 0:
                            round_late(2 * j)
                            round_late(2 * j + 1)
                            if j == 0:
                                keep_x2T(CHUNKS - 2)
                            if j == 2:
                                keep_x2T(CHUNKS - 1)
                        if first and layer == 1 and j < 2:
                            round_late(2 * HID_SLOTS + j)

            act.wait_ge(got_scales, 16)
            ffn(0, first=True)
            with act.Fori(1, CHUNKS - 1) as n:
                ffn(n)
            ffn(CHUNKS - 1, last=True)

            act.wait_ge(flag_made, 1)
            finer = act.value_load(flag[0:1, 0:1], min_val=0, max_val=1)
            with act.If(finer > 0):
                split_x_hi(0)
                with act.Fori(CHUNKS, 2 * CHUNKS - 1) as n:
                    ffn(n, base=CHUNKS)
                ffn(2 * CHUNKS - 1, base=CHUNKS, last=True)

        @block.vector
        def _(dve):
            nc.vector.memset(sT[:, :, :], 0.0).then_inc(zeros_made, 1)
            nc.vector.memset(den_pick[0:KH, :], 0.0)
            nc.vector.memset(den_pick[KH:KH + 1, :], 1.0)
            nc.vector.memset(ones[:, :], 1.0)
            nc.vector.memset(kv1[:, :, 2 * KH:2 * KH + 1], 1.0).then_inc(dve_consts, 1)

            def elu(m):
                dve.wait_ge(qkv_acted, m + 1)
                nc.vector.scalar_tensor_tensor(qT[:, :], e_qk[0:KH, :], 1.0, r_qk[0:KH, :], ALU.min, ALU.add)
                nc.vector.scalar_tensor_tensor(kT[:, :], e_qk[KH:P, :], 1.0, r_qk[KH:P, :], ALU.min, ALU.add)
                nc.vector.scalar_tensor_tensor(kv1[:, :, 0:KH], e_k[:, :, :], 1.0, r_k[:, :, :],
                                               ALU.min, ALU.add).then_inc(elu_made, 1)

            def look(g, source, c, cols):
                dve.wait_ge(w_rounded, g + 1)
                nc.vector.scalar_tensor_tensor(source[:, :], source[:, :], 1.0, W[:, bass.ds(c, cols)].bitcast(F32),
                                               ALU.mult, ALU.not_equal,
                                               accum_out=unequal[:, bass.ds(g, 1)]).then_inc(w_looked, 1)

            def look_early(n, i):
                look(2 * n + i, stage[i], (2 * n + i) * ECOLS, ECOLS)

            def look_late(i):
                look(EARLY + i, late_stage[i % 2], H2 + i * LCOLS, LCOLS)

            def moments(which, n, src, tiles=range(TT)):
                for t in tiles:
                    s = nc.vector.bn_stats(stats[:, t, :], src[:, t, :])
                s.then_inc(stats_made[which], 1)
                dve.wait_ge(dve_consts, 1)
                dve.wait_ge(stats_made[which], n + 1)
                for t in tiles:
                    s = nc.vector.bn_aggr(mv[which][:, t, :], stats[:, t, :])
                s.then_inc(mv_made[which], 1)

            def scores(n, first=False):
                dve.wait_ge(sd_done, n + 1)
                nc.vector.tensor_tensor(sT[:, :, :], s_ps, mask[:, :, :], ALU.mult).then_inc(sT_made, 1)
                if not first:
                    dve.wait_ge(state_step, (TT + 1) * n)
                    nc.vector.tensor_copy(state[:, 0, :], state[:, TT, :]).then_inc(state_step, 1)
                else:
                    nc.vector.memset(state[:, 0, :], 0.0).then_inc(state_step, 1)
                for t in range(TT):
                    dve.wait_ge(state_step, (TT + 1) * n + t + 1)
                    nc.vector.tensor_tensor(state[:, t + 1, :], delta_ps[:, t, :], state[:, t, :],
                                            ALU.add).then_inc(state_step, 1)

            def fill_mean():
                dve.wait_ge(ctx_summed, CHUNKS)
                nc.vector.tensor_reduce(ctx_sum[:, :], ctx_sums[:, :, :], axis=AX.X, op=ALU.add).then_inc(mean_step, 1)
                dve.wait_ge(mean_step, 1)
                nc.vector.tensor_scalar(ctx_mean[:, :], ctx_sum[:, :], 1.0 / SC, None, ALU.mult).then_inc(mean_step, 1)
                dve.wait_ge(mean_step, 2)
                rows = LAST_CTX * P - LAST_KEYS
                for k in range(DK):
                    s = nc.vector.tensor_copy(ctx_chunk[:, k, LAST_KEYS:LAST_CTX * P],
                                              ctx_mean[:, k:k + 1].to_broadcast([P, rows]))
                s.then_inc(tail_filled, 1)

            def second_residual(n, first=False):
                dve.wait_ge(x1_made, n + 1)
                dve.wait_ge(ub_made, n + 1)
                if not first:
                    dve.wait_ge(x2_made, n)
                nc.vector.tensor_tensor(res2[:, :, :], res1[:, :, :], ub[:, :, :], ALU.add).then_inc(res2_made, 1)

            def second_moments(n):
                dve.wait_ge(res2_made, n + 1)
                moments(1, n, res2)

            def denominators(n, last=False):
                dve.wait_ge(den_done, n + 1)
                nc.vector.tensor_scalar(den[:, :], den_ps[last], DEN_EPS, None, ALU.add).then_inc(den_step, 1)
                dve.wait_ge(den_step, 2 * n + 1)
                nc.vector.reciprocal(rden[:, :], den[:, :]).then_inc(den_step, 1)
                dve.wait_ge(den_step, 2 * n + 2)

            def first_residual(n):
                dve.wait_ge(y_done, n + 1)
                dve.wait_ge(got_xt, 16 * (n + 1))
                for t in range(TT):
                    s = nc.vector.scalar_tensor_tensor(res1[:, t, :], y_ps[:, t, :], rden[:, t:t + 1], xt[:, t, :],
                                                       ALU.mult, ALU.add)
                s.then_inc(res1_made, 1)

            def first_moments(n):
                dve.wait_ge(res1_made, n + 1)
                moments(0, n, res1)

            def chunk(n, step):
                if step:
                    look_early(n - 1, 0)
                    first_moments(n - 1)
                    look_early(n - 1, 1)
                dve.wait_ge(num_done, n + 1)
                elu(n + 1)
                if step:
                    second_residual(n - 1, first=step == 1)
                scores(n + 1)
                denominators(n)
                if step:
                    second_moments(n - 1)
                first_residual(n)

            def last_chunk(n):
                first_moments(n - 1)
                fill_mean()
                split_x_lo(0, 0)
                denominators(n, last=True)
                look_early(n - 1, 0)
                second_residual(n - 1)
                dve.wait_ge(res2_made, CHUNKS - 1)
                first_residual(n)
                second_moments(n - 1)

            def split_x_lo(n, chunk_of_x):
                dve.wait_ge(xs_hi_made, n + 1)
                nc.vector.tensor_tensor(xs[1][:, :, :], x2T_all[:, :, bass.ds(chunk_of_x * T, T)],
                                        xs[0][:, :, :].bitcast(F32), ALU.subtract).then_inc(xs_ready, 1)

            elu(0)
            dve.wait_ge(mask_made, 1)
            scores(0, first=True)
            chunk(0, 0)
            chunk(1, 1)
            with dve.Fori(2, CHUNKS - 1) as n:
                chunk(n, 2)
            last_chunk(CHUNKS - 1)

            def lo(n, tile):
                h = h1 if tile // FK != 1 else h2
                dve.wait_ge(hi_made, TILES * n + tile + 1)
                nc.vector.tensor_tensor(h[1][:, tile % FK, :], hf[tile % HF][:, :],
                                        h[0][:, tile % FK, :].bitcast(F32), ALU.subtract).then_inc(h_ready, 1)

            gates_w = W[:, W1:H1].rearrange("p (k o) -> p k o", o=F)
            hidden_w = [W[:, h:h + FK * F].rearrange("p (k o) -> p k o", o=F) for h in (H1, H2)]

            def third_norm(n, count, t0, t1, step):
                tiles = range(t0, t1)
                if step == 0:
                    resid = x2_all[:, bass.ds(n, 1), t0 * D:t1 * D].rearrange("p a (t d) -> p (a t) d", d=D)
                    nc.vector.tensor_tensor(fin[:, t0:t1, :], fin[:, t0:t1, :], resid, ALU.add).then_inc(out_added, 1)
                    dve.wait_ge(out_added, count)
                    moments(2, count - 1, fin, tiles)
                else:
                    dve.wait_ge(norm_ready[2], count)
                    for t in tiles:
                        s = nc.vector.tensor_scalar(fin[:, t, :], fin[:, t, :], mv[2][:, t, 0:1], rstd[2][:, t:t + 1],
                                                    ALU.subtract, ALU.mult)
                    s.then_inc(out_made, 1)

            def ffn(n, finer=False, first=False, last=False):
                base, extra = (CHUNKS, STORES - CHUNKS) if finer else (0, 0)

                def weights_lo(i, hi_part):
                    dve.wait_ge(got_again, 16 * (LO_PIECES * (n - base) + i + 1))
                    if i:
                        dve.wait_ge(lo_used, LO_PIECES * (n - base) + i)
                    a, b = w_again[:, :], w_lo[:, :]
                    if len(hi_part.shape) == 3:
                        a, b = (v.rearrange("p (k o) -> p k o", o=P) for v in (a, b))
                    nc.vector.tensor_tensor(b, a, hi_part.bitcast(F32), ALU.subtract).then_inc(lo_made, 1)

                for m in range(GATE_SLOTS + 1):
                    if m < GATE_SLOTS:
                        if finer:
                            weights_lo(m, gates_w[:, :, m * P:(m + 1) * P])
                        dve.wait_ge(silu_made, GATE_SLOTS * n + m + 1)
                        nc.vector.scalar_tensor_tensor(hf[m % HF][:, :], ps[:, 2 * (m % PAIRS) + 1, :],
                                                       scales[:, FK + m:FK + m + 1], hf[m % HF][:, :],
                                                       ALU.mult, ALU.mult).then_inc(gate_made, 1)
                    if m:
                        lo(n, m - 1)
                    if first and not finer and m == 1:
                        look_early(CHUNKS - 2, 1)
                if first and not finer:
                    first_moments(CHUNKS - 1)
                    look_early(CHUNKS - 1, 0)
                    look_early(CHUNKS - 1, 1)
                    second_residual(CHUNKS - 1)
                    second_moments(CHUNKS - 1)
                i = GATE_SLOTS
                for layer in range(2):
                    if layer == 1 and not last:
                        split_x_lo(n + 1, n + 1 - base)
                    for j in range(HID_SLOTS):
                        if finer:
                            for m in (2 * j, 2 * j + 1):
                                for k in (0, FK // 2):
                                    weights_lo(i, hidden_w[layer][:, k:k + FK // 2, m * P:(m + 1) * P])
                                    i += 1
                        for b in range(2):
                            lo(n, FK * (layer + 1) + 2 * j + b)
                        if first and not finer:
                            if layer == 0:
                                look_late(2 * j)
                                look_late(2 * j + 1)
                            elif j < 2:
                                look_late(2 * HID_SLOTS + j)
                        if not first and layer == 0 and j < 2:
                            third_norm(n - 1 - base, n + extra, 0, TT, step=j)
                def take_output(part, t0, t1):
                    if part == 0 and not (first and not finer):
                        dve.wait_ge(stored, 16 * (n + extra))
                    slot = SLOTS - OUT_SLOTS + t0 // 2
                    bank = 2 * (slot % PAIRS) + t0 % 2
                    whole = t1 % 2 == 0
                    if whole:
                        dve.wait_ge(slot_done, SLOTS * n + slot + 1)
                    else:
                        dve.wait_ge(tile_done, n + 1)
                    nc.vector.tensor_tensor(fin[:, t0:t1, :], ps[:, bank:bank + t1 - t0, 0:D],
                                            w3s[:, :].unsqueeze(1).to_broadcast([P, t1 - t0, D]),
                                            ALU.mult).then_inc(out_read if whole else tile_read, 1)
                    if last and whole:
                        dve.wait_ge(out_read, OUT_SLOTS * n + t0 // 2 + 1)
                    elif last:
                        dve.wait_ge(tile_read, n // CHUNKS + 1)
                    if last:
                        third_norm(n - base, n + extra + part + 1, t0, t1, step=0)

                for part, (t0, t1) in enumerate(LAST_PARTS if last else ((0, 2), (2, 4))):
                    if finer and t0 % 2 == 0:
                        for k in range(0, FK, 2):
                            weights_lo(i, W[:, W3 + k * D:W3 + (k + 2) * D])
                            i += 1
                    take_output(part, t0, t1)
                if last:
                    for part, (t0, t1) in enumerate(LAST_PARTS):
                        third_norm(n - base, n + extra + part + 1, t0, t1, step=1)

            dve.wait_ge(got_w3s, 16)
            ffn(0, first=True)
            dve.wait_ge(w_looked, PIECES)
            nc.vector.tensor_reduce(unequal_sum[:, :], unequal[:, :], axis=AX.X, op=ALU.add).then_inc(weights_looked, 1)
            with dve.Fori(1, CHUNKS - 1) as n:
                ffn(n)
            dve.wait_ge(flag_sum, 1)
            nc.vector.tensor_scalar(flag[:, :], flag_ps, 0.0, None, ALU.is_gt).then_inc(flag_made, 1)
            ffn(CHUNKS - 1, last=True)

            dve.wait_ge(flag_made, 1)
            finer = dve.value_load(flag[0:1, 0:1], min_val=0, max_val=1)
            with dve.If(finer > 0):
                split_x_lo(CHUNKS, 0)
                ffn(CHUNKS, finer=True, first=True)
                with dve.Fori(CHUNKS + 1, 2 * CHUNKS - 1) as n:
                    ffn(n, finer=True)
                ffn(2 * CHUNKS - 1, finer=True, last=True)

        @block.tensor
        def _(pe):
            def qkv(m, first=False):
                pe.wait_ge(got_xT, 16 * (m + 1))
                for k in range(DK):
                    if first and k == 1:
                        pe.wait_ge(got_xT_rest, 16)
                    nc.tensor.matmul(ps[:, QK, :], wqkv[:, k, 0:2 * KH], xT[:, k, :], start=(k == 0), stop=(k == DK - 1))
                for t in range(TT):
                    for k in range(DK):
                        mm = nc.tensor.matmul(kv_ps[:, t, :], xT[:, k, t * P:(t + 1) * P], wqkv[:, k, KH:3 * KH],
                                              start=(k == 0), stop=(k == DK - 1))
                mm.then_inc(qkv_done, 1)

            def transposes(n):
                pe.wait_ge(x2_made, n + 1)
                for k in range(DK):
                    for t in range(TT):
                        mm = nc.tensor.transpose(x2T_ps[k][:, t * P:(t + 1) * P], x2[:, t, k * P:(k + 1) * P], ident[:, :])
                mm.then_inc(tr_done, 1)

            def scores(n, first=False):
                pe.wait_ge(elu_made, n + 1)
                if not first:
                    pe.wait_ge(num_copied, n)
                for t in range(TT):
                    nc.tensor.matmul(s_ps[:, t, :], kT[:, t * P:(t + 1) * P], qT[:, t * P:(t + 1) * P], start=True, stop=True)
                for t in range(TT):
                    mm = nc.tensor.matmul(delta_ps[:, t, :], kv1[:, t, 0:KH], kv1[:, t, KH:2 * KH + 1], start=True, stop=True)
                mm.then_inc(sd_done, 1)

            def cross_attention(n, step):
                pe.wait_ge(got_ctx, 16 * (n + 1))
                if step == CHUNKS - 1:
                    pe.wait_ge(tail_filled, 1)
                if step:
                    pe.wait_ge(u_copied, n)
                    pe.wait_ge(x2T_copied, n)
                for t in range(LAST_CTX if step == CHUNKS - 1 else TT):
                    for k in range(DK):
                        mm = nc.tensor.matmul(u_ps[:, t, :], ctx_chunk[:, k, t * P:(t + 1) * P], wvo[:, k, :],
                                              start=(k == 0), stop=(k == DK - 1))
                mm.then_inc(u_done, 1)

            def chunk(n, step):
                last = step == CHUNKS - 1
                if step and not last:
                    pe.wait_ge(den_step, 2 * n - 1)
                if not last:
                    qkv(n + 1)
                pe.wait_ge(sT_made, n + 1)
                pe.wait_ge(state_step, (TT + 1) * (n + 1))
                for t in range(TT):
                    cols = slice(t * P, (t + 1) * P)
                    nc.tensor.matmul(numT_ps[:, cols], kv1[:, t, KH:2 * KH + 1], sT[:, t, :], start=True, stop=False)
                    mm = nc.tensor.matmul(numT_ps[:, cols], state[:, t, :], qT[:, cols], start=False, stop=True)
                mm.then_inc(num_done, 1)
                if not last:
                    cross_attention(n, step)
                if not last:
                    scores(n + 1)
                pe.wait_ge(num_copied, n + 1)
                for t in range(TT):
                    cols = slice(t * P, (t + 1) * P)
                    mm = nc.tensor.matmul(den_ps[last][:, t:t + 1], numT[:, cols], den_pick[:, :], start=True, stop=True)
                mm.then_inc(den_done, 1)
                if step:
                    pe.wait_ge(res1_made, n)
                for t in range(TT):
                    cols = slice(t * P, (t + 1) * P)
                    mm = nc.tensor.matmul(y_ps[:, t, :], numT[0:KH, cols], wo[:, :], start=True, stop=True)
                mm.then_inc(y_done, 1)
                if last:
                    cross_attention(n, step)
                if step >= 2 and not last:
                    pe.wait_ge(u_copied, n + 1)
                    transposes(n - 2)

            pe.sem_inc(tr_done, 1)
            pe.wait_ge(zeros_made, 1)
            for _ in range(WARM_UP):
                nc.tensor.matmul(ps[:, U_B, :], sT[:, 0, :], sT[:, :, :].rearrange("p t c -> p (t c)"), start=True, stop=True)
            pe.wait_ge(got_wqkv, 16)
            qkv(0, first=True)
            for half in range(2):
                pe.wait_ge(got_wv[half], 16)
                pe.wait_ge(got_wout[half], 16)
                for c in range(DK):
                    for k in range(half * IK // 2, (half + 1) * IK // 2):
                        mm = nc.tensor.matmul(wvo_ps[c], wv[:, k, c * P:(c + 1) * P], wout[:, k, :],
                                              start=(k == 0), stop=(k == IK - 1))
            mm.then_inc(wvo_done, 1)
            pe.wait_ge(dve_consts, 1)
            scores(0, first=True)
            pe.wait_ge(wvo_copied, 1)
            pe.wait_ge(ident_made, 1)
            pe.wait_ge(got_wo, 16)
            chunk(0, 0)
            chunk(1, 1)
            with pe.Fori(2, CHUNKS - 1) as n:
                chunk(n, 2)
            chunk(CHUNKS - 1, CHUNKS - 1)
            def ffn(n, finer=False, first=False):
                def bank(slot, b):
                    return ps[:, 2 * (slot % PAIRS) + b, :]

                def pair_free(slot):
                    if slot == 0:
                        pass
                    elif slot == 1 and first:
                        pe.wait_ge(den_step, 2 * CHUNKS - 1)
                    elif slot == 2 and first:
                        pe.wait_ge(res1_made, CHUNKS)
                    elif slot < PAIRS:
                        pe.wait_ge(out_read, OUT_SLOTS * (n - 1) + slot)
                    elif slot < PAIRS + GATE_SLOTS:
                        pe.wait_ge(gate_made, GATE_SLOTS * n + slot - PAIRS + 1)
                    else:
                        pe.wait_ge(gelu_made, 2 * FK * n + 2 * (slot - PAIRS - GATE_SLOTS + 1))

                def weights_in(pieces):
                    if first:
                        pe.wait_ge(w_rounded, pieces)

                piece = LO_PIECES * (n - CHUNKS)
                pe.wait_ge(xs_ready, n + 1)
                weights_in(-(-H1 // ECOLS))
                for m in range(GATE_SLOTS):
                    pair_free(m)
                    if finer:
                        pe.wait_ge(lo_made, piece + 1)
                        piece += 1
                        for b in range(2):
                            for k in range(DK):
                                c = (DK * b + k) * P
                                for part in range(2):
                                    mm = nc.tensor.matmul(bank(m, b), w_lo[:, c:c + P], xs[part][:, k, :],
                                                          start=(k == 0 and part == 0), stop=False)
                        mm.then_inc(lo_used, 1)
                    for b, w in enumerate((W1, W2)):
                        for k in range(DK):
                            c = w + k * F + m * P
                            for part in range(2):
                                mm = nc.tensor.matmul(bank(m, b), W[:, c:c + P], xs[part][:, k, :],
                                                      start=(k == 0 and part == 0 and not finer),
                                                      stop=(k == DK - 1 and part == 1))
                    mm.then_inc(slot_done, 1)
                    if first and m == 2:
                        pe.wait_ge(u_copied, CHUNKS)
                        transposes(CHUNKS - 3)

                for layer, (w, h) in enumerate(((H1, h1), (H2, h2))):
                    for j in range(HID_SLOTS):
                        slot = GATE_SLOTS + layer * HID_SLOTS + j
                        pair_free(slot)
                        if finer:
                            pe.wait_ge(h_ready, TILES * n + (layer + 1) * FK)
                            for b in range(2):
                                for k0 in (0, FK // 2):
                                    pe.wait_ge(lo_made, piece + 1)
                                    piece += 1
                                    for k in range(FK // 2):
                                        for part in range(2):
                                            mm = nc.tensor.matmul(bank(slot, b), w_lo[:, k * P:(k + 1) * P],
                                                                  h[part][:, k0 + k, :],
                                                                  start=(k0 + k == 0 and part == 0), stop=False)
                                    mm.then_inc(lo_used, 1)
                        for k in range(FK):
                            if j == 0:
                                pe.wait_ge(h_ready, TILES * n + layer * FK + k + 1)
                            if j == 0:
                                rows_end = w + (k + 1) * F
                                weights_in(-(-rows_end // ECOLS) if layer == 0 else EARLY + k + 1)
                            for b in range(2):
                                c = w + k * F + (2 * j + b) * P
                                for part in range(2):
                                    mm = nc.tensor.matmul(bank(slot, b), W[:, c:c + P], h[part][:, k, :],
                                                          start=(k == 0 and part == 0 and not finer),
                                                          stop=(k == FK - 1 and part == 1))
                        mm.then_inc(slot_done, 1)
                        if first and layer == 0 and j in (0, 2):
                            pe.wait_ge(x2T_copied, CHUNKS + j // 2)
                            transposes(CHUNKS - 2 + j // 2)

                weights_in(PIECES)
                for pair in range(OUT_SLOTS):
                    slot = SLOTS - OUT_SLOTS + pair
                    pair_free(slot)
                    if finer:
                        pe.wait_ge(h_ready, TILES * (n + 1))
                        for k0 in range(0, FK, 2):
                            pe.wait_ge(lo_made, piece + 1)
                            piece += 1
                            for b in range(2):
                                t = 2 * pair + b
                                for k in range(2):
                                    for part in range(2):
                                        mm = nc.tensor.matmul(bank(slot, b)[:, 0:D], h1[part][:, k0 + k, t * P:(t + 1) * P],
                                                              w_lo[:, k * D:(k + 1) * D],
                                                              start=(k0 + k == 0 and part == 0), stop=False)
                            mm.then_inc(lo_used, 1)
                    order = [(k, b) for k in range(FK) for b in range(2)]
                    for k, b in order if pair == 0 else sorted(order, key=lambda kb: kb[1]):
                        if pair == b == 0:
                            pe.wait_ge(h_ready, TILES * n + 2 * FK + k + 1)
                        t = 2 * pair + b
                        for part in range(2):
                            mm = nc.tensor.matmul(bank(slot, b)[:, 0:D], h1[part][:, k, t * P:(t + 1) * P],
                                                  W[:, W3 + k * D:W3 + (k + 1) * D],
                                                  start=(k == 0 and part == 0 and not finer),
                                                  stop=(k == FK - 1 and part == 1))
                        if pair and b == 0 and k == FK - 1:
                            mm.then_inc(tile_done, 1)
                    mm.then_inc(slot_done, 1)

            ffn(0, first=True)
            with pe.Fori(1, CHUNKS - 1) as n:
                ffn(n)
            pe.wait_ge(weights_looked, 1)
            nc.tensor.matmul(flag_ps, unequal_sum[:, :], ones[:, :], start=True, stop=True).then_inc(flag_sum, 1)
            ffn(CHUNKS - 1)
            pe.wait_ge(flag_made, 1)
            finer = pe.value_load(flag[0:1, 0:1], min_val=0, max_val=1)
            with pe.If(finer > 0):
                with pe.Fori(CHUNKS, 2 * CHUNKS) as n:
                    ffn(n, finer=True)


_IN = ["x_tok", "x_feat", "ctx_feat", "wqkv", "wo", "wv", "wout", "bout", "ffn_w", "scales", "w3s"]


def kernel(x, ctx_1024, L0_attn_Wq, L0_attn_Wk, L0_attn_Wv, L0_attn_Wo, L0_xattn_Wq, L0_xattn_Wkv, L0_xattn_Wout,
           L0_xattn_bout, L0_ffn_w1_w, L0_ffn_w1_s, L0_ffn_w2_w, L0_ffn_w2_s, L0_ffn_h1_w, L0_ffn_h1_s, L0_ffn_h2_w,
           L0_ffn_h2_s, L0_ffn_w3_w, L0_ffn_w3_s):
    import numpy as np
    import concourse.bacc as bacc
    from concourse.bass_utils import run_bass_kernel_spmd

    def features_on_partitions(a):
        a = np.asarray(a)
        return a.reshape(-1, P, a.shape[1]).transpose(1, 0, 2)

    x0 = np.asarray(x)[0]
    wkv = np.asarray(L0_xattn_Wkv)
    ffn = [L0_ffn_w1_w, L0_ffn_w2_w, L0_ffn_h1_w, L0_ffn_h2_w, L0_ffn_w3_w]
    arrays = {
        "x_tok": x0.reshape(CHUNKS, TT, P, D).transpose(0, 2, 1, 3),
        "x_feat": x0.T.reshape(DK, P, CHUNKS, T).transpose(2, 1, 0, 3),
        "ctx_feat": features_on_partitions(np.asarray(ctx_1024)[0].T),
        "wqkv": features_on_partitions(np.concatenate([np.asarray(w).T for w in (L0_attn_Wq, L0_attn_Wk, L0_attn_Wv)], axis=1)),
        "wo": np.asarray(L0_attn_Wo).T,
        "wv": features_on_partitions(wkv[:, INNER:].T),
        "wout": features_on_partitions(L0_xattn_Wout),
        "bout": np.asarray(L0_xattn_bout),
        "ffn_w": np.concatenate([features_on_partitions(np.asarray(w).T).reshape(P, -1) for w in ffn], axis=1),
        "scales": np.concatenate([np.asarray(s).reshape(FK, P).T for s in (L0_ffn_w1_s, L0_ffn_w2_s, L0_ffn_h1_s, L0_ffn_h2_s)], axis=1),
        "w3s": np.asarray(L0_ffn_w3_s),
    }
    arrays = {name: np.ascontiguousarray(a) for name, a in arrays.items()}
    nc = bacc.Bacc("TRN2", target_bir_lowering=False, num_devices=1)
    args = [nc.dram_tensor("in_" + name, arrays[name].shape, mybir.dt.from_np(arrays[name].dtype), kind="ExternalInput").ap() for name in _IN]
    out = nc.dram_tensor("layer_out", (CHUNKS, P, TT * D), F32, kind="ExternalOutput").ap()
    decoder_layer(nc, *args, out)
    r = run_bass_kernel_spmd(nc, [{"in_" + name: a for name, a in arrays.items()}], core_ids=[0])
    got = r.results[0]["layer_out"]
    return got.reshape(CHUNKS, P, TT, D).transpose(0, 2, 1, 3).reshape(1, S, D)
```
